# Optimizing a Trainium2 kernel written in Bass

```python
import numpy as np
import jax
import jax.numpy as jnp

def _softmax(x, axis=-1):
    return jax.nn.softmax(x, axis=axis)
def _gelu(x):
    return jax.nn.gelu(x, approximate=True)
def _silu(x):
    return jax.nn.silu(x)
def _sigmoid(x):
    return jax.nn.sigmoid(x)
def _layernorm(x, axis=-1, eps=1e-5):
    m = jnp.mean(x, axis=axis, keepdims=True)
    v = jnp.var(x, axis=axis, keepdims=True)
    return (x - m) / jnp.sqrt(v + eps)
def _scatter_add(tgt, idx, src, axis=0):
    return tgt.at[idx].add(src)
def _segment_sum(src, seg, n):
    return jax.ops.segment_sum(src, seg, n)

kernel_name = 'mk_metaformer_d2_conv_nhwc128_06d4ae'

def setup_inputs(seed: int = 0):
    np.random.seed(seed)
    _w = jnp.asarray
    def _rec_inputs():
        import jax
        import jax.numpy as jnp
        _gk = jax.random.key(seed)
        x = -0.0009896 + 1 * jax.random.normal(jax.random.fold_in(_gk, 1), (4, 56, 56, 128), jnp.float32)
        return x
    x = _rec_inputs()
    def _L0_conv_setup():
        import jax, jax.numpy as jnp
        import numpy as np
        DIM = 128
        NUM_HEADS = 4
        HEAD_DIM = DIM // NUM_HEADS
        KSIZE = 7
        DILATION = 1
        SCALE = HEAD_DIM ** (-0.5)

        def _rpb_bias(rpb):
            coords = np.stack(np.meshgrid(np.arange(KSIZE), np.arange(KSIZE), indexing='ij'))
            coords = coords.reshape(2, -1).T
            rel = coords - KSIZE // 2 + (KSIZE - 1)
            return rpb[:, rel[:, 0], rel[:, 1]]
        key = jax.random.key(seed)
        ks = jax.random.split(key, 6)
        B, H, W = (4, 56, 56)
        x = jax.random.normal(ks[0], (B, H, W, DIM), dtype=jnp.float32)
        qkv_w = jax.random.normal(ks[1], (3 * DIM, DIM), dtype=jnp.float32) * 0.02
        qkv_b = jnp.zeros((3 * DIM,), dtype=jnp.float32)
        rpb = jax.random.normal(ks[2], (NUM_HEADS, 2 * KSIZE - 1, 2 * KSIZE - 1), dtype=jnp.float32) * 0.02
        proj_w = jax.random.normal(ks[3], (DIM, DIM), dtype=jnp.float32) * 0.02
        proj_b = jnp.zeros((DIM,), dtype=jnp.float32)
        return {'x': x, 'qkv_w': qkv_w, 'qkv_b': qkv_b, 'rpb': rpb, 'proj_w': proj_w, 'proj_b': proj_b}
    _L0_conv_all = _L0_conv_setup()
    _L0_conv_in = {k: v for k, v in _L0_conv_all.items() if k in ('qkv_w', 'qkv_b', 'rpb', 'proj_w', 'proj_b', )}
    del _L0_conv_all

    def _L0_ffn_setup():
        import jax, jax.numpy as jnp
        import numpy as np
        PADDED_SL = 8192
        TEMPERATURE = 1.0
        SIGMA_POW = 0.25

        def _stu_conv(phi, u, n):
            b, sl, d = u.shape
            sgn = jnp.where(jnp.arange(sl) % 2 == 0, 1.0, -1.0).astype(u.dtype)
            sgn3 = sgn[None, :, None]
            Vf = jnp.fft.rfft(phi, n=n, axis=0)
            Uf_p = jnp.fft.rfft(u, n=n, axis=1)
            Uf_m = jnp.fft.rfft(u * sgn3, n=n, axis=1)
            U_plus = jnp.fft.irfft(Vf[None, :, :, None] * Uf_p[:, :, None, :], n=n, axis=1)[:, :sl]
            U_minus = jnp.fft.irfft(Vf[None, :, :, None] * Uf_m[:, :, None, :], n=n, axis=1)[:, :sl]
            U_minus = U_minus * sgn[None, :, None, None]
            return (U_plus, U_minus)

        def _compute_spectral(u, sigma, phi, Mpp, Mpm):
            U_plus, U_minus = _stu_conv(phi, u, PADDED_SL)
            s = sigma ** SIGMA_POW
            out = jnp.einsum('btkd,k,kde->bte', U_plus, s, Mpp)
            out = out + jnp.einsum('btkd,k,kde->bte', U_minus, s, Mpm)
            return out

        def _compute_ar_u(Mu, u):
            sl = u.shape[1]
            out = jnp.zeros(u.shape[:2] + (Mu.shape[-1],), dtype=u.dtype)
            for i in range(Mu.shape[0]):
                ui = jnp.pad(u, ((0, 0), (i, 0), (0, 0)))[:, :sl]
                out = out + jnp.einsum('btd,de->bte', ui, Mu[i])
            return out

        def _stu(u, sigma, phi, Mu, Mpp, Mpm):
            return _compute_spectral(u, sigma, phi, Mpp, Mpm) + _compute_ar_u(Mu, u)
        key = jax.random.key(seed)
        ks = jax.random.split(key, 8)
        b, sl, d, K, k_u = (2, 4096, 128, 16, 3)
        x = jax.random.normal(ks[0], (b, sl, d), dtype=jnp.float32)
        sigma = jax.random.uniform(ks[1], (K,), dtype=jnp.float32, minval=0.001, maxval=1.0)
        phi = jax.random.normal(ks[2], (sl, K), dtype=jnp.float32) / np.sqrt(sl)
        M_u = jax.random.normal(ks[3], (4, k_u, d, d), dtype=jnp.float32) * 0.02
        M_phi_plus = jax.random.normal(ks[4], (4, K, d, d), dtype=jnp.float32) * 0.02
        M_phi_minus = jax.random.normal(ks[5], (4, K, d, d), dtype=jnp.float32) * 0.02
        log_weights = jnp.ones((4,), dtype=jnp.float32)
        u01 = jax.random.uniform(ks[6], (4,), dtype=jnp.float32, minval=1e-06, maxval=1.0 - 1e-06)
        gumbel = -jnp.log(-jnp.log(u01))
        return {'x': x, 'sigma': sigma, 'phi': phi, 'M_u': M_u, 'M_phi_plus': M_phi_plus, 'M_phi_minus': M_phi_minus, 'log_weights': log_weights, 'gumbel': gumbel}
    _L0_ffn_all = _L0_ffn_setup()
    _L0_ffn_in = {k: v for k, v in _L0_ffn_all.items() if k in ('sigma', 'phi', 'M_u', 'M_phi_plus', 'M_phi_minus', 'log_weights', 'gumbel', )}
    del _L0_ffn_all

    def _L1_conv_setup():
        import jax, jax.numpy as jnp
        import numpy as np
        key = jax.random.key(seed)
        k1, k2, k3, k4 = jax.random.split(key, 4)
        bs, M, K, d = (64, 64, 64, 128)
        h = 128
        inputs = jax.random.normal(k1, (bs, M, K, d), dtype=jnp.float32)
        scale = float(np.sqrt(2.0 / (h + d)))
        Wself = jax.random.normal(k2, (h, d), dtype=jnp.float32) * scale
        Wm = jax.random.normal(k3, (h, d), dtype=jnp.float32) * scale
        Wk = jax.random.normal(k4, (h, d), dtype=jnp.float32) * scale
        return {'inputs': inputs, 'Wself': Wself, 'Wm': Wm, 'Wk': Wk}
    _L1_conv_all = _L1_conv_setup()
    _L1_conv_in = {k: v for k, v in _L1_conv_all.items() if k in ('Wself', 'Wm', 'Wk', )}
    del _L1_conv_all

    def _L1_ffn_setup():
        import jax, jax.numpy as jnp
        import numpy as np
        BN_EPS = 1e-05
        key = jax.random.key(seed)
        k1, k2, k3 = jax.random.split(key, 3)
        B, T, I, H = (64, 2048, 128, 128)
        x = jax.random.normal(k1, (B, T, I), dtype=jnp.float32)
        W = jax.random.normal(k2, (H, I), dtype=jnp.float32) * (1.0 / np.sqrt(I))
        V = jnp.linalg.qr(jax.random.normal(k3, (H, H), dtype=jnp.float32))[0]
        gamma = jnp.ones((H,), dtype=jnp.float32)
        beta = jnp.zeros((H,), dtype=jnp.float32)
        return {'x': x, 'W': W, 'V': V, 'gamma': gamma, 'beta': beta}
    _L1_ffn_all = _L1_ffn_setup()
    _L1_ffn_in = {k: v for k, v in _L1_ffn_all.items() if k in ('W', 'V', 'gamma', 'beta', )}
    del _L1_ffn_all

    return {
        "x": x,
        "L0_conv_qkv_w": _L0_conv_in["qkv_w"],
        "L0_conv_qkv_b": _L0_conv_in["qkv_b"],
        "L0_conv_rpb": _L0_conv_in["rpb"],
        "L0_conv_proj_w": _L0_conv_in["proj_w"],
        "L0_conv_proj_b": _L0_conv_in["proj_b"],
        "L0_ffn_sigma": _L0_ffn_in["sigma"],
        "L0_ffn_phi": _L0_ffn_in["phi"],
        "L0_ffn_M_u": _L0_ffn_in["M_u"],
        "L0_ffn_M_phi_plus": _L0_ffn_in["M_phi_plus"],
        "L0_ffn_M_phi_minus": _L0_ffn_in["M_phi_minus"],
        "L0_ffn_log_weights": _L0_ffn_in["log_weights"],
        "L0_ffn_gumbel": _L0_ffn_in["gumbel"],
        "L1_conv_Wself": _L1_conv_in["Wself"],
        "L1_conv_Wm": _L1_conv_in["Wm"],
        "L1_conv_Wk": _L1_conv_in["Wk"],
        "L1_ffn_W": _L1_ffn_in["W"],
        "L1_ffn_V": _L1_ffn_in["V"],
        "L1_ffn_gamma": _L1_ffn_in["gamma"],
        "L1_ffn_beta": _L1_ffn_in["beta"],
    }

def reference(x, L0_conv_qkv_w, L0_conv_qkv_b, L0_conv_rpb, L0_conv_proj_w, L0_conv_proj_b, L0_ffn_sigma, L0_ffn_phi, L0_ffn_M_u, L0_ffn_M_phi_plus, L0_ffn_M_phi_minus, L0_ffn_log_weights, L0_ffn_gumbel, L1_conv_Wself, L1_conv_Wm, L1_conv_Wk, L1_ffn_W, L1_ffn_V, L1_ffn_gamma, L1_ffn_beta):
    import jax
    import jax.numpy as jnp
    def _L0_conv_ref(x, qkv_w, qkv_b, rpb, proj_w, proj_b):
        import jax, jax.numpy as jnp
        import numpy as np
        DIM = 128
        NUM_HEADS = 4
        HEAD_DIM = DIM // NUM_HEADS
        KSIZE = 7
        DILATION = 1
        SCALE = HEAD_DIM ** (-0.5)

        def _rpb_bias(rpb):
            coords = np.stack(np.meshgrid(np.arange(KSIZE), np.arange(KSIZE), indexing='ij'))
            coords = coords.reshape(2, -1).T
            rel = coords - KSIZE // 2 + (KSIZE - 1)
            return rpb[:, rel[:, 0], rel[:, 1]]
        B, H, W, C = x.shape
        qkv = x @ qkv_w.T + qkv_b
        qkv = qkv.reshape(B, H, W, 3, NUM_HEADS, HEAD_DIM).transpose(3, 0, 4, 1, 2, 5)
        q, k, v = (qkv[0], qkv[1], qkv[2])
        pad = KSIZE // 2 * DILATION
        kp = jnp.pad(k, ((0, 0), (0, 0), (pad, pad), (pad, pad), (0, 0)))
        vp = jnp.pad(v, ((0, 0), (0, 0), (pad, pad), (pad, pad), (0, 0)))
        off = jnp.arange(0, KSIZE * DILATION, DILATION)
        idx_i = jnp.arange(H)[:, None] + off[None, :]
        idx_j = jnp.arange(W)[:, None] + off[None, :]
        Ai = idx_i[:, None, :, None]
        Aj = idx_j[None, :, None, :]
        k_win = kp[:, :, Ai, Aj, :].reshape(B, NUM_HEADS, H, W, KSIZE * KSIZE, HEAD_DIM)
        v_win = vp[:, :, Ai, Aj, :].reshape(B, NUM_HEADS, H, W, KSIZE * KSIZE, HEAD_DIM)
        bias = _rpb_bias(rpb)
        attn = jnp.einsum('bnhwd,bnhwkd->bnhwk', q, k_win) * SCALE
        attn = attn + bias[None, :, None, None, :]
        attn = jax.nn.softmax(attn, axis=-1)
        out = jnp.einsum('bnhwk,bnhwkd->bnhwd', attn, v_win)
        out = out.transpose(0, 2, 3, 1, 4).reshape(B, H, W, C)
        return out @ proj_w.T + proj_b

    def _L0_ffn_ref(x, sigma, phi, M_u, M_phi_plus, M_phi_minus, log_weights, gumbel):
        import jax, jax.numpy as jnp
        import numpy as np
        PADDED_SL = 8192
        TEMPERATURE = 1.0
        SIGMA_POW = 0.25

        def _stu_conv(phi, u, n):
            b, sl, d = u.shape
            sgn = jnp.where(jnp.arange(sl) % 2 == 0, 1.0, -1.0).astype(u.dtype)
            sgn3 = sgn[None, :, None]
            Vf = jnp.fft.rfft(phi, n=n, axis=0)
            Uf_p = jnp.fft.rfft(u, n=n, axis=1)
            Uf_m = jnp.fft.rfft(u * sgn3, n=n, axis=1)
            U_plus = jnp.fft.irfft(Vf[None, :, :, None] * Uf_p[:, :, None, :], n=n, axis=1)[:, :sl]
            U_minus = jnp.fft.irfft(Vf[None, :, :, None] * Uf_m[:, :, None, :], n=n, axis=1)[:, :sl]
            U_minus = U_minus * sgn[None, :, None, None]
            return (U_plus, U_minus)

        def _compute_spectral(u, sigma, phi, Mpp, Mpm):
            U_plus, U_minus = _stu_conv(phi, u, PADDED_SL)
            s = sigma ** SIGMA_POW
            out = jnp.einsum('btkd,k,kde->bte', U_plus, s, Mpp)
            out = out + jnp.einsum('btkd,k,kde->bte', U_minus, s, Mpm)
            return out

        def _compute_ar_u(Mu, u):
            sl = u.shape[1]
            out = jnp.zeros(u.shape[:2] + (Mu.shape[-1],), dtype=u.dtype)
            for i in range(Mu.shape[0]):
                ui = jnp.pad(u, ((0, 0), (i, 0), (0, 0)))[:, :sl]
                out = out + jnp.einsum('btd,de->bte', ui, Mu[i])
            return out

        def _stu(u, sigma, phi, Mu, Mpp, Mpm):
            return _compute_spectral(u, sigma, phi, Mpp, Mpm) + _compute_ar_u(Mu, u)
        T = x.shape[1]
        outs = []
        for i, frac in enumerate((1, 2, 4, 8)):
            xi = x[:, :T // frac]
            si = _stu(xi, sigma, phi, M_u[i], M_phi_plus[i], M_phi_minus[i])
            si = jnp.pad(si, ((0, 0), (0, T - si.shape[1]), (0, 0)))
            outs.append(si)
        y_soft = jax.nn.softmax((log_weights + gumbel) / TEMPERATURE)
        y_hard = jax.nn.one_hot(jnp.argmax(y_soft), 4, dtype=y_soft.dtype)
        weights = y_hard - jax.lax.stop_gradient(y_soft) + y_soft
        stacked = jnp.stack(outs, axis=-1)
        return jnp.sum(stacked * weights, axis=-1)

    def _L1_conv_ref(inputs, Wself, Wm, Wk):
        import jax, jax.numpy as jnp
        import numpy as np
        message_m = jnp.sum(inputs, axis=2)
        message_k = jnp.sum(inputs, axis=1)
        z_self = jnp.einsum('bmkd,hd->bmkh', inputs, Wself)
        z_m = jnp.einsum('bmd,hd->bmh', message_m, Wm)[:, :, None, :]
        z_k = jnp.einsum('bkd,hd->bkh', message_k, Wk)[:, None, :, :]
        return z_self + z_m + z_k

    def _L1_ffn_ref(x, W, V, gamma, beta):
        import jax, jax.numpy as jnp
        import numpy as np
        BN_EPS = 1e-05
        B, T, H = (x.shape[0], x.shape[1], W.shape[0])
        Wx = jnp.einsum('bti,hi->bth', x, W)
        flat = Wx.reshape(B * T, H)
        mean = jnp.mean(flat, axis=0)
        var = jnp.var(flat, axis=0)
        Wx = ((flat - mean) * jax.lax.rsqrt(var + BN_EPS) * gamma + beta).reshape(B, T, H)
        Vt = V.T

        def step(yt, wx_t):
            yt = jax.nn.sigmoid(wx_t + yt @ Vt)
            return (yt, yt)
        y0 = jnp.zeros((B, H), dtype=Wx.dtype)
        _, ys = jax.lax.scan(step, y0, jnp.swapaxes(Wx, 0, 1))
        return jnp.swapaxes(ys, 0, 1)

    def _gn(v, G=32, eps=1e-5):
        B_, H_, W_, C_ = v.shape
        g = v.reshape(B_, H_, W_, G, C_ // G)
        m = jnp.mean(g, axis=(1, 2, 4), keepdims=True)
        s = jnp.var(g, axis=(1, 2, 4), keepdims=True)
        return ((g - m) / jnp.sqrt(s + eps)).reshape(v.shape)

    def _ln_c(v, eps=1e-6):
        m = jnp.mean(v, axis=-1, keepdims=True)
        s = jnp.var(v, axis=-1, keepdims=True)
        return (v - m) / jnp.sqrt(s + eps)

    def _ln_t(v, eps=1e-5):
        m = jnp.mean(v, axis=-1, keepdims=True)
        s = jnp.var(v, axis=-1, keepdims=True)
        return (v - m) / jnp.sqrt(s + eps)

    def _to_tokens(v):
        B_, H_, W_, C_ = v.shape
        return v.reshape(B_, H_ * W_, C_)
    def _from_tokens(t, like):
        return t.reshape(like.shape)

    x = x + _L0_conv_ref(_ln_c(x), L0_conv_qkv_w, L0_conv_qkv_b, L0_conv_rpb, L0_conv_proj_w, L0_conv_proj_b)
    t = _to_tokens(x)
    t = t + _L0_ffn_ref(_ln_t(t), L0_ffn_sigma, L0_ffn_phi, L0_ffn_M_u, L0_ffn_M_phi_plus, L0_ffn_M_phi_minus, L0_ffn_log_weights, L0_ffn_gumbel)
    x = _from_tokens(t, x)
    x = x + _L1_conv_ref(_ln_c(x), L1_conv_Wself, L1_conv_Wm, L1_conv_Wk)
    t = _to_tokens(x)
    t = t + _L1_ffn_ref(_ln_t(t), L1_ffn_W, L1_ffn_V, L1_ffn_gamma, L1_ffn_beta)
    x = _from_tokens(t, x)
    return x


_drawn_inputs = setup_inputs


def setup_inputs(seed=0):
    import zlib

    import numpy as np

    out = dict(_drawn_inputs(seed))
    spreads = {'L0_conv_qkv_b': (0.0, 0.1),
     'L0_conv_proj_b': (0.0, 0.1),
     'L0_ffn_log_weights': (1.0, 0.2),
     'L1_ffn_gamma': (1.0, 0.6),
     'L1_ffn_beta': (0.0, 2.0)}
    factors = {'L0_conv_qkv_w': 3.815, 'L0_conv_rpb': 64.0, 'L1_ffn_W': 17.294, 'L1_ffn_V': 7.025}
    for name, (base, spread) in spreads.items():
        noise = np.random.default_rng([zlib.crc32(name.encode()), seed]).standard_normal(out[name].shape)
        drawn = base * np.exp(spread * noise) if base else spread * noise
        out[name] = jnp.asarray(drawn.astype(out[name].dtype))
    for name, factor in factors.items():
        out[name] = (out[name] * factor).astype(out[name].dtype)
    return out
```

```python
from contextlib import ExitStack

import concourse.bass as bass
from concourse import mybir

ALU = mybir.AluOpType
ACT = mybir.ActivationFunctionType
AX = mybir.AxisListType
F32 = mybir.dt.float32
F16 = mybir.dt.float16
ds = bass.ds

C = 128
B, H, W = 4, 56, 56
T = H * W
NT = B * T
CH = 448
NCH = NT // CH
CPI = T // CH
TP = 112
TPI = T // TP

XA, XV = 4 * B, 3 * B

HEADS, HD, KS, PAD = 4, 32, 7, 3
SCALE = HD ** -0.5
QR, QC = 8, 14
KR, KC = QR + KS - 1, QC + KS - 1
NK = KR * KC
HP, WP = H + 2 * PAD, W + 2 * PAD
TILES = (H // QR) * (W // QC)
KEY_CHUNKS = [(0, 6), (6, 6), (12, 2)]
ER, EC = QR + KR - 1, QC + KC - 1
OUTSIDE = -1.0e30

K, L = 16, T // 2
NB = L // TP
CC = 392
GPP = L // CC
TAPW = TP + L
EXPERTS, AR = 4, 3
U_SCALE, PHI_SCALE = 256.0, 1024.0
EIGHTHS = [3, 2, 1, 1, 0, 0, 0, 0]

ONE = 1

SB = 112
NSB = T // SB


def build(nc, x, qkv_w, qkv_b, rpb, proj_w, proj_b, sigma, phi, M_u, M_plus, M_minus, log_w, gumbel,
          Wself, Wm, Wk, Wr, Vr, gamma, beta, out):
    with ExitStack() as ctx:
        def sb(name, shape, dt=F32):
            return ctx.enter_context(nc.sbuf_tensor(name, shape, dt))

        def sem(name):
            return ctx.enter_context(nc.semaphore(name))

        bank = [ctx.enter_context(nc.psum_tensor(f"bank{i}", [C, 512], F32)) for i in range(8)]

        X = sb("X", [C, NT])
        N = sb("N", [C, NT])
        A = sb("A", [C, 14336])
        WT = sb("WT", [C, 9, C])
        ident = sb("ident", [C, C])
        mean_w = sb("mean_w", [C, C])
        ones16 = sb("ones16", [K, C])
        qkvb = sb("qkvb", [C, 3])
        projb = sb("projb", [C, 1])
        gb = sb("gb", [C, 2])
        S1 = sb("S1", [C, 4, CH])
        S2 = sb("S2", [C, 4, CH])
        Mu_eff = sb("Mu_eff", [C, 4, AR, C])
        small = sb("small", [C, 64])
        wsk = sb("wsk", [C, EXPERTS, K])
        sk = sb("sk", [C, K])
        ker = sb("ker", [K, 8])
        diag16 = sb("diag16", [K, K])
        sums = sb("sums", [C, 2, B, H])
        stats = sb("stats", [C, NCH, 6])
        bn = sb("bn", [C, 8])
        unit = sb("unit", [C, 1])
        eps = sb("eps", [C, 2])
        WORK = sb("WORK", [C, 6144])

        x_tok = A[0:TP, :].rearrange("p (b j c) -> p b j c", b=B, c=C)
        w_raw = N[:, 0:9 * C].rearrange("p (n c) -> p n c", c=C)
        phi_raw = N[0:TP, 2048:2048 + TPI * K].rearrange("p (j k) -> p j k", k=K)
        mu_raw = N[:, 4096:4096 + EXPERTS * AR * C].rearrange("p (i a e) -> p i a e", i=EXPERTS, a=AR)
        phiT = N[0:K, 6016:6016 + T]
        taps = N[0:K, 9184:9184 + 2 * TAPW].bitcast(F16).rearrange("p (h q w) -> p h q w", h=2, q=2)
        window = WORK[0:HEADS, 6144 - ER * EC:6144].rearrange("p (a b) -> p a b", a=ER)
        kpad = A[:, 0:HP * WP].rearrange("p (h w) -> p h w", h=HP)
        vpad = A[:, HP * WP:2 * HP * WP].rearrange("p (h w) -> p h w", h=HP)
        qT = A[:, 2 * HP * WP:2 * HP * WP + T].rearrange("p (t n) -> p t n", t=TILES)
        wbias = A[0:TP, 10880:10880 + HEADS * NK].rearrange("p (h k) -> p h k", h=HEADS)
        logits = [A[0:TP, 12032:12032 + HEADS * NK].rearrange("p (h k) -> p h k", h=HEADS),
                  WORK[0:TP, 0:HEADS * NK].rearrange("p (h k) -> p h k", h=HEADS)]
        probsT = WORK[:, 1152:1152 + 3 * CH].rearrange("p (c n) -> p c n", c=3)
        v_win = WORK[:, 2560:2560 + 3 * C].rearrange("p (c n) -> p c n", c=3)
        waited = WORK[0:TP, 3788:3792]
        v_chan = WORK[:, 3228:3228 + 2 * NK].rearrange("p (s k) -> p s k", s=2)
        o_tok = WORK[0:TP, 3072:3072 + C]
        amax = WORK[0:TP, 3200:3208]
        aneg = WORK[0:TP, 3208:3216]
        aden = WORK[0:TP, 3216:3224]
        arec = WORK[0:TP, 3224:3228]
        u16 = A[0:TP, :].bitcast(F16).rearrange("p (h b n q d) -> p h b n q d", h=2, b=B, q=2, n=NB)
        N16 = N[:, :].bitcast(F16)
        toep = [N16[0:TP, h * 6400:h * 6400 + 4 * (L + 1)].rearrange("p (h q w) -> p h q w", h=2, q=2)
                for h in range(2)]
        zs = N[:, 6400:6400 + 4 * CC].rearrange("p (s e n) -> p s e n", s=2, e=2)
        m_raw = [WORK[:, h * 1024:h * 1024 + 1024].rearrange("p (s i e) -> p s i e", s=2, i=EXPERTS) for h in range(2)]
        m_eff = [WORK[:, 2048 + h * 1024:3072 + h * 1024].rearrange("p (s i e) -> p s i e", s=2, i=EXPERTS) for h in range(2)]
        m_sum = WORK[:, 4096:5120].rearrange("p (s i e) -> p s i e", s=2, i=EXPERTS)
        wx = A[:, 0:NT].rearrange("p (t b) -> p t b", b=B)
        wxn = WORK[:, 0:2 * CH].rearrange("p (s n) -> p s n", s=2)
        ys = WORK[:, 896:896 + 2 * CH].rearrange("p (s n) -> p s n", s=2)
        res = WORK[:, 1792:1792 + 2 * CH].rearrange("p (s n) -> p s n", s=2)
        o_out = WORK[0:TP, 2688:2688 + 1024].rearrange("p (s b c) -> p s b c", s=2, b=B)

        WQ, WKEY, WV, WP_, WSELF, WM, WK_, WR, WV_R = range(9)

        window_d = nc.dram_tensor("window_d", [HEADS, TP, ER * EC], F32)
        taps_d = nc.dram_tensor("taps_d", [K * 4 * TAPW], F16)

        w_loaded = sem("w_loaded"); c_loaded = sem("c_loaded"); x_loaded = [sem(f"x_loaded{b}") for b in range(B)]
        phi_loaded = sem("phi_loaded"); mu_loaded = sem("mu_loaded")
        rpb_loaded = sem("rpb_loaded"); window_stored = sem("window_stored"); bias_loaded = sem("bias_loaded")
        taps_stored = sem("taps_stored")
        pool_set = sem("pool_set"); consts = sem("consts"); window_set = sem("window_set"); pads_set = sem("pads_set")
        w_turned = sem("w_turned"); w_kept = sem("w_kept")
        phi_turned = sem("phi_turned"); phi_kept = sem("phi_kept")
        taps_split = sem("taps_split"); dve_set = sem("dve_set"); exp_set = sem("exp_set")
        sk_spread = sem("sk_spread"); gates = sem("gates"); diag_set = sem("diag_set")
        x_turned = sem("x_turned"); x_kept_a = sem("x_kept_a"); x_kept_v = sem("x_kept_v")
        ln_mean = sem("ln_mean"); ln_diff = sem("ln_diff"); ln_sq = sem("ln_sq")
        root_set = sem("root_set"); ln_var = sem("ln_var"); ln_std = sem("ln_std"); ln_rstd = sem("ln_rstd"); ln_out = sem("ln_out")
        qkv_mm = sem("qkv_mm"); qv_kept = sem("qv_kept"); k_kept = sem("k_kept")
        qk_mm = sem("qk_mm"); biased = sem("biased"); max_ready = sem("max_ready"); exp_done = sem("exp_done")
        v_cut = sem("v_cut"); v_turned = sem("v_turned"); v_kept = sem("v_kept")
        p_turned = sem("p_turned"); p_kept_v = sem("p_kept_v"); p_kept_a = sem("p_kept_a")
        pv_mm = sem("pv_mm"); rec_done = sem("rec_done"); o_scaled = sem("o_scaled")
        o_turned = sem("o_turned"); o_kept = sem("o_kept"); proj_mm = sem("proj_mm"); attn_added = sem("attn_added")
        ar_mm = sem("ar_mm"); ar_added = sem("ar_added")
        u_parted = sem("u_parted"); u_turned = sem("u_turned"); u_hi = sem("u_hi"); u_lo = sem("u_lo")
        toep_loaded = [sem("toep_loaded0"), sem("toep_loaded1")]
        m_loaded = [sem("m_loaded0"), sem("m_loaded1")]
        m_summed = sem("m_summed"); m_step = sem("m_step"); m_ready = sem("m_ready")
        conv_mm = sem("conv_mm"); z_kept = sem("z_kept"); mix_mm = sem("mix_mm"); mix_added = sem("mix_added")
        sums_done = sem("sums_done"); msg_mm = sem("msg_mm"); msg_added = sem("msg_added")
        wx_mm = sem("wx_mm"); wx_stats = sem("wx_stats"); wx_kept = sem("wx_kept"); bn_step = sem("bn_step")
        wx_normed = sem("wx_normed"); wx_placed = sem("wx_placed")
        step_mm = sem("step_mm"); y_ready = sem("y_ready")
        res_added = sem("res_added"); res_turned = sem("res_turned"); res_kept = sem("res_kept")
        stored = [sem("stored0"), sem("stored1")]

        x_d = x.rearrange("b h w c -> b (h w) c").rearrange("b (j p) c -> b p j c", p=TP)
        out_d = out.rearrange("b h w c -> b (h w) c").rearrange("b t c -> t b c")

        block = ctx.enter_context(nc.Block())

        @block.sync
        def _(sp):
            for n, w in enumerate([qkv_w[0:C, :], qkv_w[C:2 * C, :], qkv_w[2 * C:3 * C, :], proj_w,
                                   Wself, Wm, Wk, Wr, Vr]):
                sp.dma_start(w_raw[:, n, :], w).then_inc(w_loaded, 16)
            for b in range(B):
                sp.dma_start(x_tok[:, b], x_d[b]).then_inc(x_loaded[b], 16)
            sp.wait_ge(window_set, 1)
            for h in range(HEADS):
                sp.dma_start(window[h:h + 1, QR - 1:QR - 1 + KS, QC - 1:QC - 1 + KS],
                             rpb[h:h + 1, PAD:PAD + KS, PAD:PAD + KS]).then_inc(rpb_loaded, 16)
            sp.wait_ge(rpb_loaded, 16 * HEADS)
            sp.dma_start(window_d.ap(), window.rearrange("p a b -> p (a b)").unsqueeze(1)
                         .broadcast_to([HEADS, TP, ER * EC])).then_inc(window_stored, 16)
            sp.wait_ge(taps_split, 1)
            sp.dma_start(taps_d.ap().rearrange("(k n) -> k n", k=K),
                         taps.rearrange("p h q w -> p (h q w)")).then_inc(taps_stored, 16)
            sp.wait_ge(window_stored, 16)
            sp.wait_ge(x_kept_a, XA)
            sp.wait_ge(x_kept_v, XV)
            for h in range(HEADS):
                for qi in range(QR):
                    src = bass.AP(window_d, (h * TP + qi * QC) * ER * EC + (QR - 1 - qi) * EC + QC - 1,
                                  [[ER * EC - 1, QC], [EC, KR], [1, KC]])
                    sp.dma_start(wbias[qi * QC:(qi + 1) * QC, h, :].rearrange("p (a b) -> p a b", a=KR),
                                 src).then_inc(bias_loaded, 16)
            sp.wait_ge(attn_added, ONE + NCH)
            sp.wait_ge(ar_mm, B * 8)
            sp.wait_ge(u_turned, ONE + B * 7)
            sp.wait_ge(taps_stored, 16)
            for k in range(K):
                half = k % 2
                if k >= 2:
                    sp.wait_ge(mix_mm, ONE + 8 * B * (k - 1))
                src = bass.AP(taps_d, k * 4 * TAPW, [[1, TP], [TAPW, 4], [1, L + 1]])
                sp.dma_start(toep[half].rearrange("p h q w -> p (h q) w"), src).then_inc(toep_loaded[half], 16)
                if k >= 2:
                    sp.wait_ge(m_summed, k - 1)
                for s, m in enumerate((M_plus, M_minus)):
                    sp.dma_start(m_raw[half][:, s], m[:, k].rearrange("i d e -> d i e")).then_inc(m_loaded[half], 16)
            with sp.Fori(0, NSB // 2) as n2:
                for s in range(2):
                    sp.wait_ge(res_kept, ONE + 2 * n2 + s + 1)
                    sp.dma_start(out_d[ds((2 * n2 + s) * SB, SB)], o_out[:, s]).then_inc(stored[s], 16)
            for s in range(2):
                sp.wait_ge(stored[s], 16 * (NSB // 2))

        @block.gpsimd
        def _(pool):
            for signal in (ln_out, res_added):
                pool.sem_inc(signal, ONE)
            pool.memset(unit[:, :], 1.0)
            pool.memset(eps[:, 0:1], 1e-6)
            pool.memset(eps[:, 1:2], 1e-5)
            pool.memset(mean_w[:, :], 1.0 / C)
            pool.memset(ones16[:, :], 1.0)
            pool.memset(ident[:, :], 0.0).then_inc(pool_set, 1)
            pool.wait_ge(pool_set, 1)
            pool.affine_select(out=ident[:, :], in_=ident[:, :], compare_op=ALU.not_equal, fill=1.0, base=0,
                               pattern=[[-1, C]], channel_multiplier=1).then_inc(consts, 1)
            pool.memset(window, OUTSIDE).then_inc(window_set, 1)
            for n in range(3):
                pool.dma_start(qkvb[:, n:n + 1], qkv_b[n * C:(n + 1) * C].rearrange("(p a) -> p a", a=1)).then_inc(c_loaded, 16)
            pool.dma_start(projb[:, :], proj_b.rearrange("(p a) -> p a", a=1)).then_inc(c_loaded, 16)
            pool.dma_start(gb[:, 0:1], gamma.rearrange("(p a) -> p a", a=1)).then_inc(c_loaded, 16)
            pool.dma_start(gb[:, 1:2], beta.rearrange("(p a) -> p a", a=1)).then_inc(c_loaded, 16)
            pool.dma_start(ker[:, 0:1], sigma.rearrange("(p a) -> p a", a=1)).then_inc(c_loaded, 16)
            pool.dma_start(small[:, 0:4], bass.AP(log_w.tensor, 0, [[0, C], [1, 4]])).then_inc(c_loaded, 16)
            pool.dma_start(small[:, 4:8], bass.AP(gumbel.tensor, 0, [[0, C], [1, 4]])).then_inc(c_loaded, 16)
            pool.dma_start(phi_raw, phi[0:T, :].rearrange("(j p) k -> p j k", p=TP)).then_inc(phi_loaded, 16)
            pool.dma_start(mu_raw, M_u.rearrange("i a d e -> d i a e")).then_inc(mu_loaded, 16)

            def norm(ln):
                with pool.Fori(0, NCH // 4) as i:
                    for u in range(4):
                        n = 4 * i + u
                        pool.wait_ge(ln_rstd, ln * NCH + n + 1)
                        pool.tensor_tensor(N[:, ds(n * CH, CH)], N[:, ds(n * CH, CH)], S2[:, u, :],
                                           ALU.mult).then_inc(ln_out, 1)

            norm(0)
            pool.wait_ge(x_kept_a, XA)
            pool.wait_ge(x_kept_v, XV)
            pool.memset(A[:, 0:2 * HP * WP], 0.0).then_inc(pads_set, 1)
            with pool.Fori(0, B) as b:
                pool.wait_ge(qv_kept, 14 * b + 14)
                for t in range(TILES):
                    r0, c0 = t // (W // QC) * QR, t % (W // QC) * QC
                    pool.wait_ge(v_turned, ONE + TILES * b + (t - 1 if t >= 2 else 0))
                    keys = vpad[:, r0:r0 + KR, c0:c0 + KC]
                    pool.tensor_tensor(v_chan[:, t % 2].rearrange("p (h w) -> p h w", h=KR), keys,
                                       unit[:, :].unsqueeze(2).broadcast_to([C, KR, KC]), ALU.mult).then_inc(v_cut, 1)
            norm(1)
            pool.wait_ge(gates, 1)

            def matrices(k, half):
                pool.wait_ge(m_loaded[half], 16 * (k - half) + 32)
                pool.tensor_tensor(m_sum[:, 0], m_raw[half][:, 0], m_raw[half][:, 1], ALU.add)
                pool.tensor_tensor(m_sum[:, 1], m_raw[half][:, 0], m_raw[half][:, 1],
                                   ALU.subtract).then_inc(m_summed, 1)
                pool.wait_ge(m_summed, k + 1)
                if not isinstance(k, int):
                    pool.wait_ge(mix_mm, ONE + 8 * B * (k - 1))
                for e in range(2):
                    last = pool.tensor_tensor(m_eff[half][:, e], m_sum[:, e],
                                              wsk[:, :, ds(k, 1)].broadcast_to([C, EXPERTS, C]), ALU.mult)
                last.then_inc(m_step, 1)
                for r in range(1, EXPERTS):
                    pool.wait_ge(m_step, 3 * k + r)
                    pool.tensor_tensor(m_eff[half][:, :, r], m_eff[half][:, :, r], m_eff[half][:, :, r - 1],
                                       ALU.add).then_inc(m_step if r < EXPERTS - 1 else m_ready, 1)

            matrices(0, 0)
            matrices(1, 1)
            with pool.Fori(1, K // 2) as k2:
                for half in range(2):
                    matrices(2 * k2 + half, half)
            norm(2)
            norm(3)
            with pool.Fori(0, NSB // 2) as n2:
                for s in range(2):
                    n = 2 * n2 + s
                    pool.wait_ge(y_ready, n * SB + SB)
                    pool.wait_ge(res_turned, ONE + n)
                    pool.tensor_tensor(res[:, s].rearrange("p (b t) -> p b t", b=B),
                                       X[:, :].rearrange("p (b t) -> p b t", b=B)[:, :, ds(n * SB, SB)],
                                       ys[:, s].rearrange("p (t b) -> p b t", b=B), ALU.add).then_inc(res_added, 1)

        @block.tensor
        def _(pe):
            for signal in (v_turned, qk_mm, p_turned, pv_mm, o_turned, u_turned, mix_mm, ln_var, res_turned):
                pe.sem_inc(signal, ONE)
            pe.wait_ge(consts, 1)
            pe.wait_ge(w_loaded, 16 * 9)
            for n in range(9):
                mm = pe.transpose(bank[n // 4][:, n % 4 * C:(n % 4 + 1) * C], w_raw[:, n, :], ident[:, :])
                if n in (3, 7, 8):
                    mm.then_inc(w_turned, 1)
            pe.wait_ge(phi_loaded, 16)
            for g in range(CPI):
                if g >= 4:
                    pe.wait_ge(phi_kept, g - 3)
                for j in range(4):
                    mm = pe.transpose(bank[3 + g % 4][0:K, j * TP:(j + 1) * TP], phi_raw[:, 4 * g + j, :],
                                      ident[0:TP, 0:TP])
                mm.then_inc(phi_turned, 1)
            pe.wait_ge(w_kept, 3)
            pe.wait_ge(phi_kept, CPI)
            for b in range(B):
                pe.wait_ge(x_loaded[b], 16)
                if b:
                    pe.wait_ge(x_kept_a, 4 * b)
                    pe.wait_ge(x_kept_v, 3 * b)
                for g in range(CPI):
                    for j in range(4):
                        mm = pe.transpose(bank[g][:, j * TP:(j + 1) * TP], x_tok[:, b, 4 * g + j, :],
                                          ident[0:TP, 0:TP])
                    mm.then_inc(x_turned, 1)
            pe.wait_ge(diag_set, 1)
            pe.matmul(bank[7][:, 0:K], ones16[:, :], diag16[:, :], start=True, stop=True).then_inc(sk_spread, 1)

            def norm(ln):
                with pe.Fori(0, NCH // 4) as i:
                    pe.wait_ge(ln_diff, ONE + ln * NCH + 4 * i)
                    for u in range(4):
                        pe.matmul(bank[u][:, 0:CH], mean_w[:, :], X[:, ds((4 * i + u) * CH, CH)],
                                  start=True, stop=True).then_inc(ln_mean, 1)
                    pe.wait_ge(ln_std, ONE + ln * NCH + 4 * i)
                    for u in range(4):
                        pe.wait_ge(ln_sq, ln * NCH + 4 * i + u + 1)
                        pe.matmul(bank[4 + u][:, 0:CH], mean_w[:, :], S1[:, u, :],
                                  start=True, stop=True).then_inc(ln_var, 1)

            pe.wait_ge(x_kept_a, XA)
            pe.wait_ge(x_kept_v, XV)
            pe.wait_ge(gates, 1)
            norm(0)

            pe.wait_ge(ln_out, ONE + NCH)
            with pe.Fori(0, B) as b:
                pe.wait_ge(attn_added, ONE + CPI * b)
                for c in range(CPI):
                    for n, w in enumerate((WQ, WKEY, WV)):
                        if c >= 2 and n == 0:
                            pe.wait_ge(qv_kept, 14 * b + 2 * c - 3)
                        if c >= 2 and n == 1:
                            pe.wait_ge(k_kept, 7 * b + c - 1)
                        if c >= 2 and n == 2:
                            pe.wait_ge(qv_kept, 14 * b + 2 * c - 2)
                        pe.matmul(bank[2 * n + c % 2][:, 0:CH], WT[:, w, :], N[:, ds(b * T + c * CH, CH)],
                                  start=True, stop=True).then_inc(qkv_mm, 1)
                pe.wait_ge(qv_kept, 14 * b + 14)
                pe.wait_ge(k_kept, 7 * b + 7)

                def scores(t):
                    r0, c0 = t // (W // QC) * QR, t % (W // QC) * QC
                    for h in range(HEADS):
                        i = HEADS * t + h
                        if i >= 3:
                            pe.wait_ge(biased, 4 * TILES * b + i - 2)
                        p = slice(h * HD, (h + 1) * HD)
                        pe.matmul(bank[i % 3][0:TP, 0:NK], qT[p, t, :],
                                  kpad[p, r0:r0 + KR, c0:c0 + KC], start=True, stop=True).then_inc(qk_mm, 1)

                def turn_out(t):
                    pe.wait_ge(o_scaled, TILES * b + t + 1)
                    pe.transpose(bank[7][:, 128:128 + TP], o_tok, ident[0:TP, 0:TP]).then_inc(o_turned, 1)

                scores(0)
                for t in range(TILES):
                    r0, c0 = t // (W // QC) * QR, t % (W // QC) * QC
                    if t + 1 < TILES:
                        scores(t + 1)
                    if t:
                        turn_out(t - 1)
                    pe.wait_ge(v_cut, TILES * b + t + 1)
                    pe.wait_ge(v_kept, ONE + TILES * b + t)
                    for c, (kr, nr) in enumerate(KEY_CHUNKS):
                        mm = pe.transpose(bank[6][0:nr * KC, c * C:(c + 1) * C],
                                          v_chan[:, t % 2, kr * KC:(kr + nr) * KC], ident[:, :])
                    mm.then_inc(v_turned, 1)
                    pe.wait_ge(exp_done, TILES * b + t + 1)
                    for c, (kr, nr) in enumerate(KEY_CHUNKS):
                        if c == 0:
                            pe.wait_ge(p_kept_v, ONE + 2 * TILES * b + 2 * t)
                            pe.wait_ge(p_kept_a, ONE + TILES * b + t)
                        for h in range(HEADS):
                            mm = pe.transpose(bank[3 + c][0:nr * KC, h * TP:(h + 1) * TP],
                                              logits[t % 2][:, h, kr * KC:(kr + nr) * KC], ident[0:TP, 0:TP])
                        mm.then_inc(p_turned, 1)
                    pe.wait_ge(p_kept_v, ONE + 2 * TILES * b + 2 * t + 2)
                    pe.wait_ge(p_kept_a, ONE + TILES * b + t + 1)
                    pe.wait_ge(v_kept, ONE + TILES * b + t + 1)
                    pe.wait_ge(o_kept, ONE + TILES * b + t)
                    for h in range(HEADS):
                        for c, (kr, nr) in enumerate(KEY_CHUNKS):
                            mm = pe.matmul(bank[7][0:TP, h * HD:(h + 1) * HD],
                                           probsT[0:nr * KC, c, h * TP:(h + 1) * TP],
                                           v_win[0:nr * KC, c, h * HD:(h + 1) * HD], start=(c == 0), stop=(c == 2))
                    mm.then_inc(pv_mm, 1)
                turn_out(TILES - 1)
                pe.wait_ge(o_kept, ONE + TILES * b + TILES)
                for c in range(CPI):
                    if c >= 2:
                        pe.wait_ge(attn_added, ONE + CPI * b + c - 1)
                    pe.matmul(bank[4 + c % 2][:, 0:CH], WT[:, WP_, :], N[:, ds(b * T + c * CH, CH)],
                              start=True, stop=True).then_inc(proj_mm, 1)

            pe.wait_ge(attn_added, ONE + NCH)
            norm(1)
            pe.wait_ge(ln_out, ONE + 2 * NCH)
            with pe.Fori(0, B) as b:
                pe.wait_ge(ar_added, ONE + 8 * b)
                for s, reach in enumerate(EIGHTHS):
                    if s >= 4:
                        pe.wait_ge(ar_added, ONE + 8 * b + s - 3)
                    for a in range(AR):
                        cut = a if s == 0 else 0
                        mm = pe.matmul(bank[s % 4][:, cut:CC], Mu_eff[:, reach, a, :],
                                       N[:, ds(b * T + s * CC - a + cut, CC - cut)],
                                       start=(a == 0), stop=(a == AR - 1))
                    mm.then_inc(ar_mm, 1)
            with pe.Fori(0, B) as b:
                for g in range(7):
                    pe.wait_ge(u_parted, 7 * b + g + 1)
                    pe.wait_ge(u_lo, ONE + 7 * b + (g - 3 if g >= 4 else 0))
                    for j in range(4):
                        mm = pe.transpose(bank[4 + g % 4][0:TP, j * C:(j + 1) * C], S1[:, g % 2, j * TP:(j + 1) * TP],
                                          ident[:, :])
                    mm.then_inc(u_turned, 1)
            pe.wait_ge(u_lo, ONE + 7 * B)
            pe.wait_ge(ar_added, ONE + 8 * B)

            with pe.Fori(0, K // 2) as k2:
                for half in range(2):
                    pe.wait_ge(toep_loaded[half], 16 * k2 + 16)
                    pe.wait_ge(m_ready, 2 * k2 + half + 1)
                    for b in range(B):
                        it = 8 * (B * (2 * k2 + half) + b)

                        def mix(g):
                            c = g % GPP
                            pe.wait_ge(z_kept, it + g + 1)
                            pe.wait_ge(mix_added, ONE + (it + g - 1 if g >= 2 else it))
                            spans = {0: [(0, CC // 2, 3), (CC // 2, CC, 2)], 1: [(0, CC, 1)]}.get(c, [(0, CC, 0)])
                            for lo, hi, reach in spans:
                                for e in range(2):
                                    mm = pe.matmul(bank[4 + g % 2][:, lo:hi], m_eff[half][:, e, reach, :],
                                                   zs[:, g % 2, e, lo:hi], start=(e == 0), stop=(e == 1))
                            mm.then_inc(mix_mm, 1)

                        for g in range(2 * GPP):
                            p, c = divmod(g, GPP)
                            if g >= 2:
                                pe.wait_ge(z_kept, it + g - 1)
                            for e in range(2):
                                q = p ^ e
                                shift = 1 if e > p else 0
                                blocks = [n for n in range(NB) if n * TP < (c + 1) * CC]
                                for n in blocks:
                                    t0 = max(c * CC, n * TP)
                                    width = (c + 1) * CC - t0
                                    tap = 1 + t0 - n * TP - shift
                                    for x, (hu, hp) in enumerate(((0, 0), (0, 1), (1, 0))):
                                        mm = pe.matmul(bank[2 * (g % 2) + e][:, t0 - c * CC:CC],
                                                       u16[:, hu, b, n, q, :],
                                                       toep[half][:, hp, e, tap:tap + width],
                                                       start=(n == 0 and x == 0), stop=(n == blocks[-1] and x == 2))
                            mm.then_inc(conv_mm, 1)
                            if g:
                                mix(g - 1)
                        mix(2 * GPP - 1)

            pe.wait_ge(mix_added, ONE + 8 * B * K)
            norm(2)
            pe.wait_ge(ln_out, ONE + 3 * NCH)
            pe.wait_ge(sums_done, 2 * B)
            for b in range(B):
                if b:
                    pe.wait_ge(msg_added, CPI * b)
                for r in range(CPI):
                    o = bank[r][:, 0:CH].rearrange("p (h w) -> p h w", w=W)
                    pe.matmul(bank[r][:, 0:CH], WT[:, WSELF, :], N[:, b * T + r * CH:b * T + (r + 1) * CH],
                              start=True, stop=False)
                    pe.matmul(o, WT[:, WM, :], sums[:, 0, b, 8 * r:8 * r + 8].unsqueeze(2).broadcast_to([C, 8, W]),
                              start=False, stop=False)
                    pe.matmul(o, WT[:, WK_, :], sums[:, 1, b, :].unsqueeze(1).broadcast_to([C, 8, W]),
                              start=False, stop=True).then_inc(msg_mm, 1)

            pe.wait_ge(msg_added, NCH)
            norm(3)
            pe.wait_ge(ln_out, ONE + 4 * NCH)
            with pe.Fori(0, B) as b:
                pe.wait_ge(wx_stats, ONE + CPI * b)
                pe.wait_ge(wx_kept, ONE + CPI * b)
                for r in range(CPI):
                    pe.matmul(bank[r][:, 0:CH], WT[:, WR, :], N[:, ds(b * T + r * CH, CH)],
                              start=True, stop=True).then_inc(wx_mm, 1)

            def place(n, s, piece):
                if piece == 0:
                    pe.wait_ge(wx_normed, n + 1)
                a = piece * CH // 4
                mm = pe.matmul(bank[s][:, a:a + CH // 4], ident[:, :], wxn[:, s, a:a + CH // 4],
                               start=(piece == 0), stop=True, skip_group_check=True)
                if piece == 3:
                    mm.then_inc(wx_placed, 1)

            def turn(n, s, b):
                if b == 0:
                    pe.wait_ge(res_added, ONE + n + 1)
                    pe.wait_ge(res_kept, ONE + n)
                mm = pe.transpose(bank[4 + s][0:SB, b * C:(b + 1) * C], res[:, s, b * SB:(b + 1) * SB], ident[:, :])
                if b == B - 1:
                    mm.then_inc(res_turned, 1)

            def steps(n, s, first, last):
                for t in range(SB):
                    prev = ys[:, s, B * t - B:B * t] if t else ys[:, 1 - s, CH - B:CH]
                    if t or not first:
                        pe.wait_ge(y_ready, n * SB + t)
                    pe.matmul(bank[s][:, B * t:B * t + B], WT[:, WV_R, :], prev,
                              start=False, stop=True, skip_group_check=True).then_inc(step_mm, 1)
                    if t % 20 == 0 and 20 <= t < 100 and not last:
                        place(n + 1, 1 - s, t // 20 - 1)
                    if t % 20 == 10 and t < 80 and not first:
                        turn(n - 1, 1 - s, t // 20)

            pe.wait_ge(wx_stats, ONE + NCH)
            pe.wait_ge(wx_kept, ONE + NCH)
            for piece in range(4):
                place(0, 0, piece)
            steps(0, 0, True, False)
            with pe.Fori(0, (NSB - 2) // 2) as n2:
                steps(2 * n2 + 1, 1, False, False)
                steps(2 * n2 + 2, 0, False, False)
            steps(NSB - 1, 1, False, True)
            for b in range(B):
                turn(NSB - 1, 1, b)

        @block.scalar
        def _(act):
            for signal in (ln_std, o_kept, v_kept, p_kept_a, wx_kept):
                act.sem_inc(signal, ONE)
            act.wait_ge(c_loaded, 16 * 9)
            act.wait_ge(consts, 1)
            act.activation(ker[:, 5:6], ker[:, 0:1], ACT.Sqrt).then_inc(root_set, 1)
            act.wait_ge(root_set, 1)
            act.activation(ker[:, 5:6], ker[:, 5:6], ACT.Sqrt).then_inc(root_set, 1)
            act.wait_ge(dve_set, 3)
            act.activation(small[:, 20:24], small[:, 16:20], ACT.Exp).then_inc(exp_set, 1)

            for b in range(B):
                for g in range(0, CPI, 2):
                    act.wait_ge(x_turned, 7 * b + g + 1)
                    act.copy(X[:, b * T + g * CH:b * T + (g + 1) * CH], bank[g][:, 0:CH]).then_inc(x_kept_a, 1)
            def norm(ln, j):
                with act.Fori(0, NCH // 4) as i:
                    act.wait_ge(ln_var, ONE + ln * NCH + 4 * i)
                    for u in range(4):
                        n = 4 * i + u
                        act.wait_ge(ln_diff, ONE + ln * NCH + n + 1)
                        act.activation(S1[:, u, :], N[:, ds(n * CH, CH)], ACT.Square).then_inc(ln_sq, 1)
                    act.wait_ge(ln_out, ONE + ln * NCH + 4 * i)
                    for u in range(4):
                        act.wait_ge(ln_var, ONE + ln * NCH + 4 * i + u + 1)
                        act.activation(S2[:, u, :], bank[4 + u][:, 0:CH], ACT.Sqrt, bias=eps[:, j:j + 1]).then_inc(ln_std, 1)

            norm(0, 0)

            act.wait_ge(pads_set, 1)
            with act.Fori(0, B) as b:
                act.wait_ge(qk_mm, ONE + 4 * TILES * b)
                for c in range(CPI):
                    act.wait_ge(qkv_mm, 21 * b + 3 * c + 2)
                    act.activation(kpad[:, PAD + 8 * c:PAD + 8 * c + 8, PAD:PAD + W],
                                   bank[2 + c % 2][:, 0:CH].rearrange("p (h w) -> p h w", w=W),
                                   ACT.Identity, bias=qkvb[:, 1:2]).then_inc(k_kept, 1)

                def exps(t):
                    s = t % 2
                    act.wait_ge(max_ready, TILES * b + t + 1)
                    act.wait_ge(rec_done, ONE + (TILES * b + t - 1 if t >= 2 else TILES * b))
                    for h in range(HEADS):
                        last = act.activation(logits[s][:, h, :], logits[s][:, h, :], ACT.Exp,
                                              bias=aneg[:, 4 * s + h:4 * s + h + 1],
                                              accum_out=aden[:, 4 * s + h:4 * s + h + 1])
                    last.then_inc(exp_done, 1)

                def keep_out(t):
                    r0, c0 = t // (W // QC) * QR, t % (W // QC) * QC
                    act.wait_ge(o_turned, ONE + TILES * b + t + 1)
                    act.copy(N[:, :].rearrange("p (b h w) -> p b h w", b=B, h=H)[:, ds(b, 1), r0:r0 + QR, c0:c0 + QC],
                             bank[7][:, 128:128 + TP].rearrange("p (b h w) -> p b h w", b=1, h=QR)
                             ).then_inc(o_kept, 1)

                exps(0)
                for t in range(TILES):
                    if t:
                        keep_out(t - 1)
                    act.wait_ge(v_turned, ONE + TILES * b + t + 1)
                    act.wait_ge(pv_mm, ONE + TILES * b + t)
                    act.copy(v_win[0:120, 0:2, :].rearrange("p c n -> p (c n)"), bank[6][0:120, 0:2 * C])
                    act.copy(v_win[0:40, 2, :], bank[6][0:40, 2 * C:3 * C]).then_inc(v_kept, 1)
                    act.wait_ge(p_turned, ONE + 3 * TILES * b + 3 * t + 3)
                    act.copy(probsT[0:40, 2, :], bank[5][0:40, 0:CH]).then_inc(p_kept_a, 1)
                    if t + 1 < TILES:
                        exps(t + 1)
                keep_out(TILES - 1)

            norm(1, 1)
            act.wait_ge(ln_out, ONE + 2 * NCH)
            with act.Fori(0, B) as b:
                def part(g):
                    act.wait_ge(u_turned, ONE + 7 * b + (g - 1 if g >= 2 else 0))
                    backwards = bass.AP(S1, g % 2 * CH + TP - 1, [[4 * CH, C], [2 * TP, 2], [TP, 2], [-1, TP]])
                    act.copy(backwards, N[:, ds(b * T + g * CH, CH)].rearrange("p (n i q) -> p n q i", n=2, q=2)
                             ).then_inc(u_parted, 1)

                def high(g):
                    act.wait_ge(u_turned, ONE + 7 * b + g + 1)
                    act.activation(u16[:, 0, ds(b, 1)].rearrange("p b n q d -> p (b n q d)")[:, g * 512:(g + 1) * 512],
                                   bank[4 + g % 4][0:TP, :], ACT.Copy, scale=U_SCALE).then_inc(u_hi, 1)

                part(0)
                for g in range(7):
                    if g < 6:
                        part(g + 1)
                    high(g)
            with act.Fori(0, K * B) as it8:
                it = 8 * it8
                for g in range(8):
                    act.wait_ge(conv_mm, it + g + 1)
                    act.wait_ge(mix_mm, ONE + (it + g - 1 if g >= 2 else it))
                    act.copy(zs[:, g % 2, 0, :], bank[2 * (g % 2)][:, 0:CC])
                    act.copy(zs[:, g % 2, 1, :], bank[2 * (g % 2) + 1][:, 0:CC]).then_inc(z_kept, 1)

            norm(2, 0)
            norm(3, 1)
            with act.Fori(0, B) as b:
                for r in range(CPI):
                    act.wait_ge(wx_mm, CPI * b + r + 1)
                    act.copy(wx[:, r * CH:(r + 1) * CH, ds(b, 1)],
                             bank[r][:, 0:CH].unsqueeze(2)).then_inc(wx_kept, 1)

            act.wait_ge(bn_step, 1)
            act.activation(bn[:, 2:3], bn[:, 1:2], ACT.Sqrt, bias=eps[:, 1:2]).then_inc(bn_step, 1)

            def steps(n, s):
                if not (isinstance(n, int) and n == 0):
                    act.wait_ge(res_added, ONE + n - 1)
                for t in range(SB):
                    act.wait_ge(step_mm, n * SB + t + 1)
                    act.activation(ys[:, s, B * t:B * t + B], bank[s][:, B * t:B * t + B],
                                   ACT.Sigmoid).then_inc(y_ready, 1)

            steps(0, 0)
            with act.Fori(0, (NSB - 2) // 2) as n2:
                steps(2 * n2 + 1, 1)
                steps(2 * n2 + 2, 0)
            steps(NSB - 1, 1)

        @block.vector
        def _(dve):
            for signal in (ln_diff, attn_added, p_kept_v, ar_added, u_lo, mix_added, wx_stats, rec_done, res_kept):
                dve.sem_inc(signal, ONE)
            count = [0]

            def link(ins):
                count[0] += 1
                ins.then_inc(dve_set, 1)
                dve.wait_ge(dve_set, count[0])

            dve.wait_ge(c_loaded, 16 * 9)
            link(dve.tensor_tensor(small[:, 8:12], small[:, 0:4], small[:, 4:8], ALU.add))
            link(dve.tensor_reduce(small[:, 12:13], small[:, 8:12], AX.X, ALU.max))
            link(dve.tensor_scalar(small[:, 16:20], small[:, 8:12], small[:, 12:13], None, ALU.subtract))
            for n in range(3):
                k = 4 if n < 2 else 1
                dve.wait_ge(w_turned, n + 1)
                dve.tensor_copy(WT[:, 4 * n:4 * n + k, :].rearrange("p n c -> p (n c)"),
                                bank[n][:, 0:k * C]).then_inc(w_kept, 1)
            for g in range(CPI):
                dve.wait_ge(phi_turned, g + 1)
                dve.tensor_copy(phiT[:, g * CH:(g + 1) * CH], bank[3 + g % 4][0:K, 0:CH]).then_inc(phi_kept, 1)
            dve.wait_ge(phi_kept, CPI)
            link(dve.memset(taps[:, :, :, 0:TP], 0.0))
            link(dve.tensor_reduce(ker[:, 1:2], phiT, AX.X, ALU.max, apply_absolute_value=True))
            link(dve.tensor_scalar(ker[:, 2:3], ker[:, 1:2], 1e-30, None, ALU.max))
            link(dve.reciprocal(ker[:, 3:4], ker[:, 2:3]))
            link(dve.tensor_scalar(ker[:, 4:5], ker[:, 3:4], PHI_SCALE, None, ALU.mult))
            for q in range(2):
                link(dve.tensor_scalar(taps[:, 0, q, TP:], phiT[:, q::2], ker[:, 4:5], None, ALU.mult))
            for q in range(2):
                last = dve.scalar_tensor_tensor(out=taps[:, 1, q, TP:], in0=phiT[:, q::2], scalar=ker[:, 4:5],
                                                in1=taps[:, 0, q, TP:], op0=ALU.mult, op1=ALU.subtract)
            last.then_inc(taps_split, 1)
            dve.wait_ge(root_set, 2)
            link(dve.tensor_scalar(ker[:, 6:7], ker[:, 2:3], 1.0 / (PHI_SCALE * U_SCALE), None, ALU.mult))
            link(dve.tensor_tensor(ker[:, 7:8], ker[:, 5:6], ker[:, 6:7], ALU.mult))
            dve.wait_ge(consts, 1)
            dve.tensor_scalar(diag16[:, :], ident[0:K, 0:K], ker[:, 7:8], None, ALU.mult).then_inc(diag_set, 1)
            for b in range(B):
                for g in range(1, CPI, 2):
                    dve.wait_ge(x_turned, 7 * b + g + 1)
                    dve.tensor_copy(X[:, b * T + g * CH:b * T + (g + 1) * CH], bank[g][:, 0:CH]).then_inc(x_kept_v, 1)
            dve.wait_ge(sk_spread, 1)
            link(dve.tensor_copy(sk[:, :], bank[7][:, 0:K]))
            dve.wait_ge(exp_set, 1)
            link(dve.tensor_reduce(small[:, 24:25], small[:, 20:24], AX.X, ALU.add))
            link(dve.reciprocal(small[:, 25:26], small[:, 24:25]))
            link(dve.tensor_scalar(small[:, 28:32], small[:, 20:24], small[:, 25:26], None, ALU.mult))
            link(dve.tensor_reduce(small[:, 32:33], small[:, 28:32], AX.X, ALU.max))
            link(dve.tensor_scalar(small[:, 36:40], small[:, 28:32], small[:, 32:33], None, ALU.is_equal))
            link(dve.tensor_scalar(small[:, 40:44], small[:, 36:40], -1.0, 1.0, ALU.mult, ALU.add))
            link(dve.memset(small[:, 44:45], 1.0))
            for i in range(1, EXPERTS):
                link(dve.tensor_tensor(small[:, 44 + i:45 + i], small[:, 43 + i:44 + i], small[:, 39 + i:40 + i], ALU.mult))
            link(dve.tensor_tensor(small[:, 48:52], small[:, 36:40], small[:, 44:48], ALU.mult))
            link(dve.tensor_tensor(small[:, 52:56], small[:, 48:52], small[:, 28:32], ALU.subtract))
            link(dve.tensor_tensor(small[:, 56:60], small[:, 52:56], small[:, 28:32], ALU.add))
            for i in range(EXPERTS):
                dve.tensor_scalar(wsk[:, i, :], sk[:, :], small[:, 56 + i:57 + i], None, ALU.mult)
            dve.wait_ge(mu_loaded, 16)
            link(dve.tensor_scalar(Mu_eff[:, 0], mu_raw[:, 0], small[:, 56:57], None, ALU.mult))
            for i in range(1, EXPERTS):
                link(dve.scalar_tensor_tensor(out=Mu_eff[:, i], in0=mu_raw[:, i], scalar=small[:, 56 + i:57 + i],
                                              in1=Mu_eff[:, i - 1], op0=ALU.mult, op1=ALU.add))
            dve.memset(bn[:, 7:8], 0.0).then_inc(gates, 1)

            def norm(ln):
                with dve.Fori(0, NCH // 4) as i:
                    for u in range(4):
                        n = 4 * i + u
                        dve.wait_ge(ln_mean, ln * NCH + n + 1)
                        dve.tensor_tensor(N[:, ds(n * CH, CH)], X[:, ds(n * CH, CH)], bank[u][:, 0:CH],
                                          ALU.subtract).then_inc(ln_diff, 1)
                    for u in range(4):
                        dve.wait_ge(ln_std, ONE + ln * NCH + 4 * i + u + 1)
                        dve.reciprocal(S2[:, u, :], S2[:, u, :]).then_inc(ln_rstd, 1)

            dve.wait_ge(taps_stored, 16)
            norm(0)

            dve.wait_ge(pads_set, 1)
            dve.wait_ge(bias_loaded, 16 * HEADS * QR)
            with dve.Fori(0, B) as b:
                dve.wait_ge(qk_mm, ONE + 4 * TILES * b)
                dve.wait_ge(v_turned, ONE + TILES * b)
                for c in range(CPI):
                    dve.wait_ge(qkv_mm, 21 * b + 3 * c + 1)
                    dve.tensor_scalar(qT[:, 4 * c:4 * c + 4, :].rearrange("p t (i j) -> p i t j", i=QR),
                                      bank[c % 2][:, 0:CH].rearrange("p (i t j) -> p i t j", i=QR, t=4),
                                      qkvb[:, 0:1], SCALE, ALU.add, ALU.mult).then_inc(qv_kept, 1)
                    dve.wait_ge(qkv_mm, 21 * b + 3 * c + 3)
                    dve.tensor_scalar(vpad[:, PAD + 8 * c:PAD + 8 * c + 8, PAD:PAD + W],
                                      bank[4 + c % 2][:, 0:CH].rearrange("p (h w) -> p h w", w=W),
                                      qkvb[:, 2:3], None, ALU.add).then_inc(qv_kept, 1)

                def row_max(t):
                    s = t % 2
                    dve.wait_ge(p_turned, ONE + 3 * TILES * b + (3 * t - 3 if t >= 2 else 0))
                    for h in range(HEADS):
                        dve.wait_ge(qk_mm, ONE + 4 * TILES * b + 4 * t + h + 1)
                        dve.memset(waited[:, h:h + 1], 0.0)
                        dve.tensor_tensor_reduce(out=logits[s][:, h, :], in0=bank[(HEADS * t + h) % 3][0:TP, 0:NK], in1=wbias[:, h, :],
                                                 scale=1.0, scalar=-3.0e38, op0=ALU.add, op1=ALU.max,
                                                 accum_out=amax[:, 4 * s + h:4 * s + h + 1]).then_inc(biased, 1)
                    dve.wait_ge(biased, 4 * TILES * b + 4 * t + 4)
                    dve.tensor_scalar(aneg[:, 4 * s:4 * s + 4], amax[:, 4 * s:4 * s + 4], -1.0, None,
                                      ALU.mult).then_inc(max_ready, 1)

                row_max(0)
                for t in range(TILES):
                    s = t % 2
                    if t + 1 < TILES:
                        row_max(t + 1)
                    dve.wait_ge(pv_mm, ONE + TILES * b + t)
                    for c in range(2):
                        dve.wait_ge(p_turned, ONE + 3 * TILES * b + 3 * t + c + 1)
                        dve.tensor_copy(probsT[0:120, c, :], bank[3 + c][0:120, 0:CH]).then_inc(p_kept_v, 1)
                    dve.wait_ge(exp_done, TILES * b + t + 1)
                    dve.reciprocal(arec, aden[:, 4 * s:4 * s + 4]).then_inc(rec_done, 1)
                    dve.wait_ge(rec_done, ONE + TILES * b + t + 1)
                    dve.wait_ge(pv_mm, ONE + TILES * b + t + 1)
                    dve.wait_ge(o_turned, ONE + TILES * b + t)
                    dve.tensor_tensor(o_tok.rearrange("p (h d) -> p h d", h=HEADS),
                                      bank[7][0:TP, 0:C].rearrange("p (h d) -> p h d", h=HEADS),
                                      arec.unsqueeze(2).broadcast_to([TP, HEADS, HD]), ALU.mult).then_inc(o_scaled, 1)
                for c in range(CPI):
                    dve.wait_ge(proj_mm, CPI * b + c + 1)
                    xs = X[:, ds(b * T + c * CH, CH)]
                    dve.scalar_tensor_tensor(out=xs, in0=bank[4 + c % 2][:, 0:CH], scalar=projb[:, 0:1], in1=xs,
                                             op0=ALU.add, op1=ALU.add).then_inc(attn_added, 1)

            norm(1)
            with dve.Fori(0, B) as b:
                for s in range(8):
                    dve.wait_ge(ar_mm, 8 * b + s + 1)
                    xs = X[:, ds(b * T + s * CC, CC)]
                    dve.tensor_tensor(xs, xs, bank[s % 4][:, 0:CC], ALU.add).then_inc(ar_added, 1)
            with dve.Fori(0, B) as b:
                for g in range(7):
                    dve.wait_ge(u_hi, 7 * b + g + 1)
                    hi, lo = (u16[:, h, ds(b, 1)].rearrange("p b n q d -> p (b n q d)")[:, g * 512:(g + 1) * 512]
                              for h in range(2))
                    dve.scalar_tensor_tensor(out=lo, in0=bank[4 + g % 4][0:TP, :], scalar=U_SCALE, in1=hi,
                                             op0=ALU.mult, op1=ALU.subtract).then_inc(u_lo, 1)
            with dve.Fori(0, K) as k:
                with dve.Fori(0, B) as b:
                    it = 8 * (B * k + b)
                    for g in range(8):
                        p, c = divmod(g, GPP)
                        dve.wait_ge(mix_mm, ONE + it + g + 1)
                        xs = X[:, :].rearrange("p (b t q) -> p b t q", b=B, q=2)[:, ds(b, 1), c * CC:(c + 1) * CC, p]
                        dve.tensor_tensor(xs, xs, bank[4 + g % 2][:, 0:CC].unsqueeze(1),
                                          ALU.add).then_inc(mix_added, 1)

            norm(2)
            dve.wait_ge(ln_out, ONE + 3 * NCH)
            grid = N[:, :].rearrange("p (b h w) -> p b h w", b=B, h=H)
            for b in range(B):
                dve.tensor_reduce(sums[:, 0, b, :], grid[:, b], AX.X, ALU.add).then_inc(sums_done, 1)
                dve.tensor_reduce(sums[:, 1, b, :], grid[:, b].rearrange("p h w -> p w h"), AX.X,
                                  ALU.add).then_inc(sums_done, 1)
            with dve.Fori(0, B) as b:
                for r in range(CPI):
                    dve.wait_ge(msg_mm, CPI * b + r + 1)
                    xs = X[:, ds(b * T + r * CH, CH)]
                    dve.tensor_tensor(xs, xs, bank[r][:, 0:CH], ALU.add).then_inc(msg_added, 1)

            norm(3)
            with dve.Fori(0, B) as b:
                for r in range(CPI):
                    dve.wait_ge(wx_kept, ONE + CPI * b + r + 1)
                    dve.bn_stats(stats[:, ds(CPI * b + r, 1), :], bank[r][:, 0:CH]).then_inc(wx_stats, 1)
            dve.wait_ge(wx_stats, ONE + NCH)
            dve.bn_aggr(bn[:, 0:2], stats[:, :, :].rearrange("p n s -> p (n s)")).then_inc(bn_step, 1)
            dve.wait_ge(bn_step, 2)
            link(dve.reciprocal(bn[:, 6:7], bn[:, 2:3]))
            link(dve.tensor_tensor(bn[:, 3:4], gb[:, 0:1], bn[:, 6:7], ALU.mult))
            link(dve.tensor_tensor(bn[:, 4:5], bn[:, 0:1], bn[:, 3:4], ALU.mult))
            link(dve.tensor_tensor(bn[:, 5:6], gb[:, 1:2], bn[:, 4:5], ALU.subtract))
            link(dve.memset(ys[:, 1, CH - B:CH], 0.0))
            dve.wait_ge(wx_kept, ONE + NCH)

            def scaled(n, s):
                dve.tensor_scalar(wxn[:, s, :].rearrange("p (t b) -> p t b", b=B), wx[:, ds(n * SB, SB), :],
                                  bn[:, 3:4], bn[:, 5:6], ALU.mult, ALU.add).then_inc(wx_normed, 1)

            def keep(m, s):
                dve.wait_ge(res_turned, ONE + m + 1)
                if not (isinstance(m, int) and m < 2):
                    dve.wait_ge(stored[s], 8 * (m - s))
                dve.tensor_copy(o_out[:, s].rearrange("p b c -> p (b c)"), bank[4 + s][0:SB, :]).then_inc(res_kept, 1)

            scaled(0, 0)
            scaled(1, 1)
            for n in range(2):
                dve.wait_ge(wx_placed, n + 1)
                scaled(n + 2, n)
                keep(n, n)
            with dve.Fori(1, (NSB - 2) // 2) as n2:
                for s in range(2):
                    n = 2 * n2 + s
                    dve.wait_ge(wx_placed, n + 1)
                    scaled(n + 2, s)
                    keep(n, s)
            keep(NSB - 2, 0)
            keep(NSB - 1, 1)


_INS = ["x", "L0_conv_qkv_w", "L0_conv_qkv_b", "L0_conv_rpb", "L0_conv_proj_w", "L0_conv_proj_b", "L0_ffn_sigma",
        "L0_ffn_phi", "L0_ffn_M_u", "L0_ffn_M_phi_plus", "L0_ffn_M_phi_minus", "L0_ffn_log_weights", "L0_ffn_gumbel",
        "L1_conv_Wself", "L1_conv_Wm", "L1_conv_Wk", "L1_ffn_W", "L1_ffn_V", "L1_ffn_gamma", "L1_ffn_beta"]


def kernel(**inputs):
    import numpy as _np
    import concourse.bacc as _bacc
    from concourse import mybir as _mybir
    from concourse.bass_utils import run_bass_kernel_spmd as _run

    nc = _bacc.Bacc("TRN2", target_bir_lowering=False, num_devices=1)
    arrays, args = {}, []
    for name in _INS:
        a = _np.ascontiguousarray(inputs[name])
        arrays[f"in_{name}_dram"] = a
        args.append(nc.dram_tensor(f"in_{name}_dram", a.shape, _mybir.dt.from_np(a.dtype), kind="ExternalInput").ap())
    args.append(nc.dram_tensor("out_0_dram", (B, H, W, C), F32, kind="ExternalOutput").ap())
    build(nc, *args)
    r = _run(nc, [arrays], core_ids=[0])
    return r.results[0]["out_0_dram"]
```

```python
from contextlib import ExitStack

import concourse.bass as bass
from concourse import mybir

ALU = mybir.AluOpType
ACT = mybir.ActivationFunctionType
AX = mybir.AxisListType
F32 = mybir.dt.float32
F16 = mybir.dt.float16
ds = bass.ds

C = 128
B, H, W = 4, 56, 56
T = H * W
NT = B * T
CH = 448
NCH = NT // CH
CPI = T // CH
TP = 112
TPI = T // TP

XA, XV = 4 * B, 3 * B

HEADS, HD, KS, PAD = 4, 32, 7, 3
SCALE = HD ** -0.5
QR, QC = 8, 14
KR, KC = QR + KS - 1, QC + KS - 1
NK = KR * KC
HP, WP = H + 2 * PAD, W + 2 * PAD
TILES = (H // QR) * (W // QC)
KEY_CHUNKS = [(0, 6), (6, 6), (12, 2)]
ER, EC = QR + KR - 1, QC + KC - 1
OUTSIDE = -1.0e30

K, L = 16, T // 2
NB = -(-L // C)
TAIL = L - (NB - 1) * C
UG = T // (4 * C)
CC = 392
GPP = L // CC
TAPW = C + L
EXPERTS, AR = 4, 3
U_SCALE, PHI_SCALE = 256.0, 1024.0
EIGHTHS = [3, 2, 1, 1, 0, 0, 0, 0]

ONE = 1

SB = 112
NSB = T // SB


def build(nc, x, qkv_w, qkv_b, rpb, proj_w, proj_b, sigma, phi, M_u, M_plus, M_minus, log_w, gumbel,
          Wself, Wm, Wk, Wr, Vr, gamma, beta, out):
    with ExitStack() as ctx:
        def sb(name, shape, dt=F32):
            return ctx.enter_context(nc.sbuf_tensor(name, shape, dt))

        def sem(name):
            return ctx.enter_context(nc.semaphore(name))

        bank = [ctx.enter_context(nc.psum_tensor(f"bank{i}", [C, 512], F32)) for i in range(8)]

        X = sb("X", [C, NT])
        N = sb("N", [C, NT])
        A = sb("A", [C, 14336])
        WT = sb("WT", [C, 9, C])
        ident = sb("ident", [C, C])
        mean_w = sb("mean_w", [C, C])
        mean32_w = sb("mean32_w", [C, C])
        ones16 = sb("ones16", [K, C])
        qkvb = sb("qkvb", [C, 3])
        projb = sb("projb", [C, 1])
        gb = sb("gb", [C, 2])
        S1 = sb("S1", [C, 4, CH])
        S2 = sb("S2", [C, 2, CH])
        Mu_eff = sb("Mu_eff", [C, 4, AR, C])
        small = sb("small", [C, 64])
        wsk = sb("wsk", [C, EXPERTS, K])
        sk = sb("sk", [C, K])
        ker = sb("ker", [K, 8])
        diag16 = sb("diag16", [K, K])
        sums = sb("sums", [C, 2, B, H])
        stats = sb("stats", [C, NCH, 6])
        bn = sb("bn", [C, 8])
        unit = sb("unit", [C, 1])
        eps = sb("eps", [C, 2])
        WORK = sb("WORK", [C, 6144])

        x_tok = A[0:TP, :].rearrange("p (b j c) -> p b j c", b=B, c=C)
        w_raw = N[:, 0:9 * C].rearrange("p (n c) -> p n c", c=C)
        phi_raw = N[0:TP, 2048:2048 + TPI * K].rearrange("p (j k) -> p j k", k=K)
        mu_raw = N[:, 4096:4096 + EXPERTS * AR * C].rearrange("p (i a e) -> p i a e", i=EXPERTS, a=AR)
        phiT = N[0:K, 5760:5760 + T]
        taps = N[0:K, 9152:9152 + 2 * TAPW].bitcast(F16).rearrange("p (h q w) -> p h q w", h=2, q=2)
        window = WORK[0:HEADS, 6144 - ER * EC:6144].rearrange("p (a b) -> p a b", a=ER)
        kpad = A[:, 0:HP * WP].rearrange("p (h w) -> p h w", h=HP)
        vpad = A[:, HP * WP:2 * HP * WP].rearrange("p (h w) -> p h w", h=HP)
        qT = A[:, 2 * HP * WP:2 * HP * WP + T].rearrange("p (t n) -> p t n", t=TILES)
        wbias = A[0:TP, 10880:10880 + HEADS * NK].rearrange("p (h k) -> p h k", h=HEADS)
        logits = [A[0:TP, 12032:12032 + HEADS * NK].rearrange("p (h k) -> p h k", h=HEADS),
                  WORK[0:TP, 0:HEADS * NK].rearrange("p (h k) -> p h k", h=HEADS)]
        probsT = WORK[:, 1152:1152 + 6 * CH].rearrange("p (s c n) -> p s c n", s=2, c=3)
        v_win = WORK[:, 3840:3840 + 6 * C].rearrange("p (s c n) -> p s c n", s=2, c=3)
        amax = WORK[0:TP, 4608:4616]
        aneg = WORK[0:TP, 4616:4624]
        aden = WORK[0:TP, 4624:4632]
        arec = WORK[0:TP, 4632:4636]
        waited = WORK[0:TP, 4636:4640]
        v_chan = WORK[:, 4640:4640 + 2 * NK].rearrange("p (s k) -> p s k", s=2)
        diag = WORK[0:TP, 5200:5200 + 2 * CH].rearrange("p (s h q) -> p s h q", s=2, h=HEADS)
        u16 = A[:, 0:B * NB * 2 * C].bitcast(F16).rearrange("p (h b n q d) -> p h b n q d", h=2, b=B, q=2, n=NB)
        u_part = S1[:, :, :].rearrange("p a n -> p (a n)")[:, 0:1024].rearrange("p (s n) -> p s n", s=2)
        N16 = N[:, :].bitcast(F16)
        toep = [N16[:, h * 6400:h * 6400 + 4 * (L + 1)].rearrange("p (h q w) -> p h q w", h=2, q=2)
                for h in range(2)]
        zs = N[:, 6400:6400 + 4 * CC].rearrange("p (s e n) -> p s e n", s=2, e=2)
        m_raw = [WORK[:, h * 1024:h * 1024 + 1024].rearrange("p (s i e) -> p s i e", s=2, i=EXPERTS) for h in range(2)]
        m_eff = [WORK[:, 2048 + h * 1024:3072 + h * 1024].rearrange("p (s i e) -> p s i e", s=2, i=EXPERTS) for h in range(2)]
        m_sum = WORK[:, 4096:5120].rearrange("p (s i e) -> p s i e", s=2, i=EXPERTS)
        wx = A[:, 0:NT].rearrange("p (t b) -> p t b", b=B)
        wxn = WORK[:, 0:2 * CH].rearrange("p (s n) -> p s n", s=2)
        ys = WORK[:, 896:896 + 2 * CH].rearrange("p (s n) -> p s n", s=2)
        res = WORK[:, 1792:1792 + 2 * CH].rearrange("p (s n) -> p s n", s=2)
        o_out = WORK[0:TP, 2688:2688 + 1024].rearrange("p (s b c) -> p s b c", s=2, b=B)

        WQ, WKEY, WV, WP_, WSELF, WM, WK_, WR, WV_R = range(9)

        window_d = nc.dram_tensor("window_d", [HEADS, TP, ER * EC], F32)
        taps_d = nc.dram_tensor("taps_d", [K * 4 * TAPW], F16)

        w_loaded = sem("w_loaded"); c_loaded = sem("c_loaded"); x_loaded = [sem(f"x_loaded{b}") for b in range(B)]
        phi_loaded = sem("phi_loaded"); mu_loaded = sem("mu_loaded")
        rpb_loaded = sem("rpb_loaded"); window_stored = sem("window_stored"); bias_loaded = sem("bias_loaded")
        taps_stored = sem("taps_stored")
        pool_set = sem("pool_set"); consts = sem("consts"); window_set = sem("window_set"); pads_set = sem("pads_set")
        w_turned = sem("w_turned"); w_kept = sem("w_kept")
        phi_turned = sem("phi_turned"); phi_kept = sem("phi_kept")
        taps_split = sem("taps_split"); dve_set = sem("dve_set"); exp_set = sem("exp_set")
        sk_spread = sem("sk_spread"); gates = sem("gates"); diag_set = sem("diag_set")
        x_turned = sem("x_turned"); x_kept_a = sem("x_kept_a"); x_kept_v = sem("x_kept_v")
        ln_mean = sem("ln_mean"); ln_diff = sem("ln_diff"); ln_sq = sem("ln_sq")
        root_set = sem("root_set"); ln_var = sem("ln_var"); ln_std = sem("ln_std"); ln_rstd = sem("ln_rstd"); ln_spread = sem("ln_spread"); ln_out = sem("ln_out")
        qkv_mm = sem("qkv_mm"); qv_kept = sem("qv_kept"); k_kept = sem("k_kept")
        qk_mm = sem("qk_mm"); biased = sem("biased"); max_ready = sem("max_ready"); exp_done = sem("exp_done")
        v_cut = sem("v_cut"); v_turned = sem("v_turned"); v_kept = sem("v_kept")
        p_turned = sem("p_turned"); p_kept_v = sem("p_kept_v"); p_kept_a = sem("p_kept_a")
        pv_mm = sem("pv_mm"); rec_done = sem("rec_done"); diag_ready = sem("diag_ready")
        o_kept = sem("o_kept"); proj_mm = sem("proj_mm"); attn_added = sem("attn_added")
        ar_mm = sem("ar_mm"); ar_added = sem("ar_added")
        u_parted = sem("u_parted"); u_turned = sem("u_turned"); u_hi = sem("u_hi"); u_lo = sem("u_lo")
        toep_loaded = [sem("toep_loaded0"), sem("toep_loaded1")]
        m_loaded = [sem("m_loaded0"), sem("m_loaded1")]
        m_summed = sem("m_summed"); m_step = sem("m_step"); m_ready = sem("m_ready")
        conv_mm = sem("conv_mm"); z_kept = sem("z_kept"); mix_mm = sem("mix_mm"); mix_added = sem("mix_added")
        sums_done = sem("sums_done"); msg_mm = sem("msg_mm"); msg_added = sem("msg_added")
        wx_mm = sem("wx_mm"); wx_stats = sem("wx_stats"); wx_kept = sem("wx_kept"); bn_step = sem("bn_step")
        wx_normed = sem("wx_normed"); wx_placed = sem("wx_placed")
        step_mm = sem("step_mm"); y_ready = sem("y_ready")
        res_added = sem("res_added"); res_turned = sem("res_turned"); res_kept = sem("res_kept")
        stored = [sem("stored0"), sem("stored1")]

        x_d = x.rearrange("b h w c -> b (h w) c").rearrange("b (j p) c -> b p j c", p=TP)
        out_d = out.rearrange("b h w c -> b (h w) c").rearrange("b t c -> t b c")

        block = ctx.enter_context(nc.Block())

        @block.sync
        def _(sp):
            for n, w in enumerate([qkv_w[0:C, :], qkv_w[C:2 * C, :], qkv_w[2 * C:3 * C, :], proj_w,
                                   Wself, Wm, Wk, Wr, Vr]):
                sp.dma_start(w_raw[:, n, :], w).then_inc(w_loaded, 16)
            for b in range(B):
                sp.dma_start(x_tok[:, b], x_d[b]).then_inc(x_loaded[b], 16)
            sp.wait_ge(window_set, 1)
            for h in range(HEADS):
                sp.dma_start(window[h:h + 1, QR - 1:QR - 1 + KS, QC - 1:QC - 1 + KS],
                             rpb[h:h + 1, PAD:PAD + KS, PAD:PAD + KS]).then_inc(rpb_loaded, 16)
            sp.wait_ge(rpb_loaded, 16 * HEADS)
            sp.dma_start(window_d.ap(), window.rearrange("p a b -> p (a b)").unsqueeze(1)
                         .broadcast_to([HEADS, TP, ER * EC])).then_inc(window_stored, 16)
            sp.wait_ge(taps_split, 1)
            sp.dma_start(taps_d.ap().rearrange("(k n) -> k n", k=K),
                         taps.rearrange("p h q w -> p (h q w)")).then_inc(taps_stored, 16)
            sp.wait_ge(window_stored, 16)
            sp.wait_ge(x_kept_a, XA)
            sp.wait_ge(x_kept_v, XV)
            for h in range(HEADS):
                for qi in range(QR):
                    src = bass.AP(window_d, (h * TP + qi * QC) * ER * EC + (QR - 1 - qi) * EC + QC - 1,
                                  [[ER * EC - 1, QC], [EC, KR], [1, KC]])
                    sp.dma_start(wbias[qi * QC:(qi + 1) * QC, h, :].rearrange("p (a b) -> p a b", a=KR),
                                 src).then_inc(bias_loaded, 16)
            sp.wait_ge(attn_added, ONE + NCH)
            sp.wait_ge(ar_mm, B * 8)
            sp.wait_ge(u_turned, ONE + B * 7)
            sp.wait_ge(taps_stored, 16)
            for k in range(K):
                half = k % 2
                if k >= 2:
                    sp.wait_ge(mix_mm, ONE + 8 * B * (k - 1))
                src = bass.AP(taps_d, k * 4 * TAPW, [[1, C], [TAPW, 4], [1, L + 1]])
                sp.dma_start(toep[half].rearrange("p h q w -> p (h q) w"), src).then_inc(toep_loaded[half], 16)
                if k >= 2:
                    sp.wait_ge(m_summed, k - 1)
                for s, m in enumerate((M_plus, M_minus)):
                    sp.dma_start(m_raw[half][:, s], m[:, k].rearrange("i d e -> d i e")).then_inc(m_loaded[half], 16)
            with sp.Fori(0, NSB // 2) as n2:
                for s in range(2):
                    sp.wait_ge(res_kept, ONE + 2 * n2 + s + 1)
                    sp.dma_start(out_d[ds((2 * n2 + s) * SB, SB)], o_out[:, s]).then_inc(stored[s], 16)
            for s in range(2):
                sp.wait_ge(stored[s], 16 * (NSB // 2))

        @block.gpsimd
        def _(pool):
            for signal in (res_added,):
                pool.sem_inc(signal, ONE)
            pool.memset(unit[:, :], 1.0)
            pool.memset(eps[:, 0:1], 1e-6)
            pool.memset(eps[:, 1:2], 1e-5)
            pool.memset(mean_w[:, :], 1.0 / C)
            pool.memset(mean32_w[:, :], 1.0 / 32)
            pool.memset(ones16[:, :], 1.0)
            pool.memset(ident[:, :], 0.0).then_inc(pool_set, 1)
            pool.wait_ge(pool_set, 1)
            pool.affine_select(out=ident[:, :], in_=ident[:, :], compare_op=ALU.not_equal, fill=1.0, base=0,
                               pattern=[[-1, C]], channel_multiplier=1).then_inc(consts, 1)
            pool.memset(window, OUTSIDE).then_inc(window_set, 1)
            for n in range(3):
                pool.dma_start(qkvb[:, n:n + 1], qkv_b[n * C:(n + 1) * C].rearrange("(p a) -> p a", a=1)).then_inc(c_loaded, 16)
            pool.dma_start(projb[:, :], proj_b.rearrange("(p a) -> p a", a=1)).then_inc(c_loaded, 16)
            pool.dma_start(gb[:, 0:1], gamma.rearrange("(p a) -> p a", a=1)).then_inc(c_loaded, 16)
            pool.dma_start(gb[:, 1:2], beta.rearrange("(p a) -> p a", a=1)).then_inc(c_loaded, 16)
            pool.dma_start(ker[:, 0:1], sigma.rearrange("(p a) -> p a", a=1)).then_inc(c_loaded, 16)
            pool.dma_start(small[:, 0:4], bass.AP(log_w.tensor, 0, [[0, C], [1, 4]])).then_inc(c_loaded, 16)
            pool.dma_start(small[:, 4:8], bass.AP(gumbel.tensor, 0, [[0, C], [1, 4]])).then_inc(c_loaded, 16)
            pool.dma_start(phi_raw, phi[0:T, :].rearrange("(j p) k -> p j k", p=TP)).then_inc(phi_loaded, 16)
            pool.dma_start(mu_raw, M_u.rearrange("i a d e -> d i a e")).then_inc(mu_loaded, 16)

            pool.wait_ge(x_kept_a, XA)
            pool.wait_ge(x_kept_v, XV)
            pool.memset(A[:, 0:2 * HP * WP], 0.0).then_inc(pads_set, 1)
            with pool.Fori(0, B) as b:
                pool.wait_ge(qv_kept, 14 * b + 14)
                for t in range(TILES):
                    r0, c0 = t // (W // QC) * QR, t % (W // QC) * QC
                    pool.wait_ge(v_turned, ONE + TILES * b + (t - 1 if t >= 2 else 0))
                    keys = vpad[:, r0:r0 + KR, c0:c0 + KC]
                    pool.tensor_tensor(v_chan[:, t % 2].rearrange("p (h w) -> p h w", h=KR), keys,
                                       unit[:, :].unsqueeze(2).broadcast_to([C, KR, KC]), ALU.mult).then_inc(v_cut, 1)
            pool.wait_ge(gates, 1)

            def matrices(k, half):
                pool.wait_ge(m_loaded[half], 16 * (k - half) + 32)
                pool.tensor_tensor(m_sum[:, 0], m_raw[half][:, 0], m_raw[half][:, 1], ALU.add)
                pool.tensor_tensor(m_sum[:, 1], m_raw[half][:, 0], m_raw[half][:, 1],
                                   ALU.subtract).then_inc(m_summed, 1)
                pool.wait_ge(m_summed, k + 1)
                if not isinstance(k, int):
                    pool.wait_ge(mix_mm, ONE + 8 * B * (k - 1))
                for e in range(2):
                    last = pool.tensor_tensor(m_eff[half][:, e], m_sum[:, e],
                                              wsk[:, :, ds(k, 1)].broadcast_to([C, EXPERTS, C]), ALU.mult)
                last.then_inc(m_step, 1)
                for r in range(1, EXPERTS):
                    pool.wait_ge(m_step, 3 * k + r)
                    pool.tensor_tensor(m_eff[half][:, :, r], m_eff[half][:, :, r], m_eff[half][:, :, r - 1],
                                       ALU.add).then_inc(m_step if r < EXPERTS - 1 else m_ready, 1)

            matrices(0, 0)
            matrices(1, 1)
            with pool.Fori(1, K // 2) as k2:
                for half in range(2):
                    matrices(2 * k2 + half, half)
            with pool.Fori(0, NSB // 2) as n2:
                for s in range(2):
                    n = 2 * n2 + s
                    pool.wait_ge(y_ready, n * SB + SB)
                    pool.wait_ge(res_turned, ONE + n)
                    pool.tensor_tensor(res[:, s].rearrange("p (b t) -> p b t", b=B),
                                       X[:, :].rearrange("p (b t) -> p b t", b=B)[:, :, ds(n * SB, SB)],
                                       ys[:, s].rearrange("p (t b) -> p b t", b=B), ALU.add).then_inc(res_added, 1)

        @block.tensor
        def _(pe):
            for signal in (v_turned, qk_mm, p_turned, pv_mm, u_turned, mix_mm, ln_var, res_turned):
                pe.sem_inc(signal, ONE)
            pe.wait_ge(consts, 1)
            pe.wait_ge(w_loaded, 16 * 9)
            for n in range(9):
                mm = pe.transpose(bank[n // 4][:, n % 4 * C:(n % 4 + 1) * C], w_raw[:, n, :], ident[:, :])
                if n in (3, 7, 8):
                    mm.then_inc(w_turned, 1)
            pe.wait_ge(phi_loaded, 16)
            for g in range(CPI):
                if g >= 4:
                    pe.wait_ge(phi_kept, g - 3)
                for j in range(4):
                    mm = pe.transpose(bank[3 + g % 4][0:K, j * TP:(j + 1) * TP], phi_raw[:, 4 * g + j, :],
                                      ident[0:TP, 0:TP])
                mm.then_inc(phi_turned, 1)
            pe.wait_ge(w_kept, 3)
            pe.wait_ge(phi_kept, CPI)
            for b in range(B):
                pe.wait_ge(x_loaded[b], 16)
                if b:
                    pe.wait_ge(x_kept_a, 4 * b)
                    pe.wait_ge(x_kept_v, 3 * b)
                for g in range(CPI):
                    for j in range(4):
                        mm = pe.transpose(bank[g][:, j * TP:(j + 1) * TP], x_tok[:, b, 4 * g + j, :],
                                          ident[0:TP, 0:TP])
                    mm.then_inc(x_turned, 1)
            pe.wait_ge(diag_set, 1)
            pe.matmul(bank[7][:, 0:K], ones16[:, :], diag16[:, :], start=True, stop=True).then_inc(sk_spread, 1)

            def norm(ln):
                def means(i):
                    pe.wait_ge(ln_diff, ONE + ln * NCH + 4 * i)
                    for u in range(4):
                        pe.matmul(bank[u][:, 0:CH], mean_w[:, :], X[:, ds((4 * i + u) * CH, CH)],
                                  start=True, stop=True).then_inc(ln_mean, 1)

                def variances(i):
                    for u in range(4):
                        pe.wait_ge(ln_sq, ln * NCH + 4 * i + u + 1)
                        mm = pe.matmul(bank[4][32 * u:32 * u + 32, 0:CH], mean_w[:, 0:32], S1[:, u, :],
                                       start=True, stop=True)
                    mm.then_inc(ln_var, 1)

                def spread(i):
                    pe.wait_ge(ln_rstd, ONE + ln * NCH // 4 + i + 1)
                    for u in range(4):
                        if u == 3:
                            pe.wait_ge(ln_out, ONE + ln * NCH + 4 * i + 1)
                        pe.matmul(bank[5 + u % 3][:, 0:CH], mean32_w[32 * u:32 * u + 32, :],
                                  S2[32 * u:32 * u + 32, 1, :], start=True, stop=True).then_inc(ln_spread, 1)

                means(0)
                with pe.Fori(0, NCH // 4 - 1) as i:
                    variances(i)
                    means(i + 1)
                    spread(i)
                variances(NCH // 4 - 1)
                spread(NCH // 4 - 1)

            pe.wait_ge(x_kept_a, XA)
            pe.wait_ge(x_kept_v, XV)
            pe.wait_ge(gates, 1)
            norm(0)

            pe.wait_ge(ln_out, ONE + NCH)
            with pe.Fori(0, B) as b:
                pe.wait_ge(attn_added, ONE + CPI * b)
                for c in range(CPI):
                    for n, w in enumerate((WQ, WKEY, WV)):
                        if c >= 2 and n == 0:
                            pe.wait_ge(qv_kept, 14 * b + 2 * c - 3)
                        if c >= 2 and n == 1:
                            pe.wait_ge(k_kept, 7 * b + c - 1)
                        if c >= 2 and n == 2:
                            pe.wait_ge(qv_kept, 14 * b + 2 * c - 2)
                        pe.matmul(bank[2 * n + c % 2][:, 0:CH], WT[:, w, :], N[:, ds(b * T + c * CH, CH)],
                                  start=True, stop=True).then_inc(qkv_mm, 1)
                pe.wait_ge(qv_kept, 14 * b + 14)
                pe.wait_ge(k_kept, 7 * b + 7)

                def scores(t):
                    r0, c0 = t // (W // QC) * QR, t % (W // QC) * QC
                    for h in range(HEADS):
                        i = HEADS * t + h
                        if i >= 3:
                            pe.wait_ge(biased, 4 * TILES * b + i - 2)
                        p = slice(h * HD, (h + 1) * HD)
                        pe.matmul(bank[i % 3][0:TP, 0:NK], qT[p, t, :],
                                  kpad[p, r0:r0 + KR, c0:c0 + KC], start=True, stop=True).then_inc(qk_mm, 1)

                def turn_values(t):
                    pe.wait_ge(v_cut, TILES * b + t + 1)
                    pe.wait_ge(v_kept, ONE + TILES * b + t)
                    for c, (kr, nr) in enumerate(KEY_CHUNKS):
                        mm = pe.transpose(bank[6][0:nr * KC, c * C:(c + 1) * C],
                                          v_chan[:, t % 2, kr * KC:(kr + nr) * KC], ident[:, :])
                    mm.then_inc(v_turned, 1)

                def turn_probs(t):
                    pe.wait_ge(diag_ready, TILES * b + t + 1)
                    pe.wait_ge(p_kept_v, ONE + 2 * TILES * b + 2 * t)
                    pe.wait_ge(p_kept_a, ONE + TILES * b + t)
                    for c, (kr, nr) in enumerate(KEY_CHUNKS):
                        for h in range(HEADS):
                            mm = pe.matmul(bank[3 + c][0:nr * KC, h * TP:(h + 1) * TP],
                                           logits[t % 2][:, h, kr * KC:(kr + nr) * KC], diag[:, t % 2, h, :],
                                           start=True, stop=True)
                        mm.then_inc(p_turned, 1)

                def outputs(t):
                    pe.wait_ge(p_kept_v, ONE + 2 * TILES * b + 2 * t + 2)
                    pe.wait_ge(p_kept_a, ONE + TILES * b + t + 1)
                    pe.wait_ge(v_kept, ONE + TILES * b + t + 1)
                    pe.wait_ge(o_kept, ONE + TILES * b + t)
                    for c, (kr, nr) in enumerate(KEY_CHUNKS):
                        for h in range(HEADS):
                            mm = pe.matmul(bank[7][h * HD:(h + 1) * HD, 0:TP],
                                           v_win[0:nr * KC, t % 2, c, h * HD:(h + 1) * HD],
                                           probsT[0:nr * KC, t % 2, c, h * TP:(h + 1) * TP],
                                           start=(c == 0), stop=(c == 2), skip_group_check=True)
                    mm.then_inc(pv_mm, 1)

                scores(0)
                for t in range(TILES):
                    if t + 1 < TILES:
                        scores(t + 1)
                    turn_values(t)
                    if t:
                        outputs(t - 1)
                    turn_probs(t)
                outputs(TILES - 1)
                pe.wait_ge(o_kept, ONE + TILES * b + TILES)
                for c in range(CPI):
                    if c >= 2:
                        pe.wait_ge(attn_added, ONE + CPI * b + c - 1)
                    pe.matmul(bank[4 + c % 2][:, 0:CH], WT[:, WP_, :], N[:, ds(b * T + c * CH, CH)],
                              start=True, stop=True).then_inc(proj_mm, 1)

            pe.wait_ge(attn_added, ONE + NCH)
            norm(1)
            pe.wait_ge(ln_out, ONE + 2 * NCH)
            with pe.Fori(0, B) as b:
                pe.wait_ge(ar_added, ONE + 8 * b)
                for s, reach in enumerate(EIGHTHS):
                    if s >= 4:
                        pe.wait_ge(ar_added, ONE + 8 * b + s - 3)
                    for a in range(AR):
                        cut = a if s == 0 else 0
                        mm = pe.matmul(bank[s % 4][:, cut:CC], Mu_eff[:, reach, a, :],
                                       N[:, ds(b * T + s * CC - a + cut, CC - cut)],
                                       start=(a == 0), stop=(a == AR - 1))
                    mm.then_inc(ar_mm, 1)
            with pe.Fori(0, B) as b:
                for g in range(UG + 1):
                    n = C if g < UG else TAIL
                    pe.wait_ge(u_parted, 7 * b + g + 1)
                    pe.wait_ge(u_lo, ONE + 7 * b + (g - 3 if g >= 4 else 0))
                    for j in range(4 if g < UG else 2):
                        mm = pe.transpose(bank[4 + g % 4][0:n, j * C:(j + 1) * C], u_part[:, g % 2, j * n:(j + 1) * n],
                                          ident[:, :])
                    mm.then_inc(u_turned, 1)
            pe.wait_ge(u_lo, ONE + 7 * B)
            pe.wait_ge(ar_added, ONE + 8 * B)

            with pe.Fori(0, K // 2) as k2:
                for half in range(2):
                    pe.wait_ge(toep_loaded[half], 16 * k2 + 16)
                    pe.wait_ge(m_ready, 2 * k2 + half + 1)
                    for b in range(B):
                        it = 8 * (B * (2 * k2 + half) + b)

                        def mix(g):
                            c = g % GPP
                            pe.wait_ge(z_kept, it + g + 1)
                            pe.wait_ge(mix_added, ONE + (it + g - 1 if g >= 2 else it))
                            spans = {0: [(0, CC // 2, 3), (CC // 2, CC, 2)], 1: [(0, CC, 1)]}.get(c, [(0, CC, 0)])
                            for lo, hi, reach in spans:
                                for e in range(2):
                                    mm = pe.matmul(bank[4 + g % 2][:, lo:hi], m_eff[half][:, e, reach, :],
                                                   zs[:, g % 2, e, lo:hi], start=(e == 0), stop=(e == 1))
                            mm.then_inc(mix_mm, 1)

                        for g in range(2 * GPP):
                            p, c = divmod(g, GPP)
                            if g >= 2:
                                pe.wait_ge(z_kept, it + g - 1)
                            for e in range(2):
                                q = p ^ e
                                shift = 1 if e > p else 0
                                blocks = [n for n in range(NB) if n * C < (c + 1) * CC]
                                for n in blocks:
                                    t0 = max(c * CC, n * C)
                                    width = (c + 1) * CC - t0
                                    tap = 1 + t0 - n * C - shift
                                    rows = C
                                    if n == NB - 1:
                                        rows, tap = TAIL, tap + C - TAIL
                                    for x, (hu, hp) in enumerate(((0, 0), (0, 1), (1, 0))):
                                        mm = pe.matmul(bank[2 * (g % 2) + e][:, t0 - c * CC:CC],
                                                       u16[0:rows, hu, b, n, q, :],
                                                       toep[half][0:rows, hp, e, tap:tap + width],
                                                       start=(n == 0 and x == 0), stop=(n == blocks[-1] and x == 2))
                            mm.then_inc(conv_mm, 1)
                            if g:
                                mix(g - 1)
                        mix(2 * GPP - 1)

            pe.wait_ge(mix_added, ONE + 8 * B * K)
            norm(2)
            pe.wait_ge(ln_out, ONE + 3 * NCH)
            pe.wait_ge(sums_done, 2 * B)
            for b in range(B):
                if b:
                    pe.wait_ge(msg_added, CPI * b)
                for r in range(CPI):
                    o = bank[r][:, 0:CH].rearrange("p (h w) -> p h w", w=W)
                    pe.matmul(bank[r][:, 0:CH], WT[:, WSELF, :], N[:, b * T + r * CH:b * T + (r + 1) * CH],
                              start=True, stop=False)
                    pe.matmul(o, WT[:, WM, :], sums[:, 0, b, 8 * r:8 * r + 8].unsqueeze(2).broadcast_to([C, 8, W]),
                              start=False, stop=False)
                    pe.matmul(o, WT[:, WK_, :], sums[:, 1, b, :].unsqueeze(1).broadcast_to([C, 8, W]),
                              start=False, stop=True).then_inc(msg_mm, 1)

            pe.wait_ge(msg_added, NCH)
            norm(3)
            pe.wait_ge(ln_out, ONE + 4 * NCH)
            with pe.Fori(0, B) as b:
                pe.wait_ge(wx_stats, ONE + CPI * b)
                pe.wait_ge(wx_kept, ONE + CPI * b)
                for r in range(CPI):
                    pe.matmul(bank[r][:, 0:CH], WT[:, WR, :], N[:, ds(b * T + r * CH, CH)],
                              start=True, stop=True).then_inc(wx_mm, 1)

            def place(n, s, piece):
                if piece == 0:
                    pe.wait_ge(wx_normed, n + 1)
                a = piece * CH // 4
                mm = pe.matmul(bank[s][:, a:a + CH // 4], ident[:, :], wxn[:, s, a:a + CH // 4],
                               start=(piece == 0), stop=True, skip_group_check=True)
                if piece == 3:
                    mm.then_inc(wx_placed, 1)

            def turn(n, s, b):
                if b == 0:
                    pe.wait_ge(res_added, ONE + n + 1)
                    pe.wait_ge(res_kept, ONE + n)
                mm = pe.transpose(bank[4 + s][0:SB, b * C:(b + 1) * C], res[:, s, b * SB:(b + 1) * SB], ident[:, :])
                if b == B - 1:
                    mm.then_inc(res_turned, 1)

            def steps(n, s, first, last):
                for t in range(SB):
                    prev = ys[:, s, B * t - B:B * t] if t else ys[:, 1 - s, CH - B:CH]
                    if t or not first:
                        pe.wait_ge(y_ready, n * SB + t)
                    for o in range(0, C, C // 2):
                        mm = pe.matmul(bank[s][o:o + C // 2, B * t:B * t + B], WT[:, WV_R, o:o + C // 2], prev,
                                       start=False, stop=True, skip_group_check=True)
                    mm.then_inc(step_mm, 1)
                    if t % 20 == 0 and 20 <= t < 100 and not last:
                        place(n + 1, 1 - s, t // 20 - 1)
                    if t % 20 == 10 and t < 80 and not first:
                        turn(n - 1, 1 - s, t // 20)

            pe.wait_ge(wx_stats, ONE + NCH)
            pe.wait_ge(wx_kept, ONE + NCH)
            for piece in range(4):
                place(0, 0, piece)
            steps(0, 0, True, False)
            with pe.Fori(0, (NSB - 2) // 2) as n2:
                steps(2 * n2 + 1, 1, False, False)
                steps(2 * n2 + 2, 0, False, False)
            steps(NSB - 1, 1, False, True)
            for b in range(B):
                turn(NSB - 1, 1, b)

        @block.scalar
        def _(act):
            for signal in (o_kept, v_kept, p_kept_a, wx_kept):
                act.sem_inc(signal, ONE)
            act.wait_ge(c_loaded, 16 * 9)
            act.wait_ge(consts, 1)
            act.activation(ker[:, 5:6], ker[:, 0:1], ACT.Sqrt).then_inc(root_set, 1)
            act.wait_ge(root_set, 1)
            act.activation(ker[:, 5:6], ker[:, 5:6], ACT.Sqrt).then_inc(root_set, 1)
            act.wait_ge(dve_set, 3)
            act.activation(small[:, 20:24], small[:, 16:20], ACT.Exp).then_inc(exp_set, 1)

            for b in range(B):
                for g in range(0, CPI, 2):
                    act.wait_ge(x_turned, 7 * b + g + 1)
                    act.copy(X[:, b * T + g * CH:b * T + (g + 1) * CH], bank[g][:, 0:CH]).then_inc(x_kept_a, 1)
            def norm(ln, j):
                def squares(i):
                    act.wait_ge(ln_var, ONE + ln * NCH // 4 + i)
                    for u in range(4):
                        n = 4 * i + u
                        act.wait_ge(ln_diff, ONE + ln * NCH + n + 1)
                        act.activation(S1[:, u, :], N[:, ds(n * CH, CH)], ACT.Square).then_inc(ln_sq, 1)

                def deviations(i):
                    act.wait_ge(ln_rstd, ONE + ln * NCH // 4 + i)
                    act.wait_ge(ln_var, ONE + ln * NCH // 4 + i + 1)
                    act.activation(S2[:, 0, :], bank[4][:, 0:CH], ACT.Sqrt, bias=eps[:, j:j + 1]).then_inc(ln_std, 1)

                squares(0)
                with act.Fori(0, NCH // 4 - 1) as i:
                    deviations(i)
                    squares(i + 1)
                deviations(NCH // 4 - 1)

            norm(0, 0)

            act.wait_ge(pads_set, 1)
            with act.Fori(0, B) as b:
                act.wait_ge(qk_mm, ONE + 4 * TILES * b)
                for c in range(CPI):
                    act.wait_ge(qkv_mm, 21 * b + 3 * c + 2)
                    act.activation(kpad[:, PAD + 8 * c:PAD + 8 * c + 8, PAD:PAD + W],
                                   bank[2 + c % 2][:, 0:CH].rearrange("p (h w) -> p h w", w=W),
                                   ACT.Identity, bias=qkvb[:, 1:2]).then_inc(k_kept, 1)

                def exps(t):
                    s = t % 2
                    act.wait_ge(max_ready, TILES * b + t + 1)
                    act.wait_ge(rec_done, ONE + (TILES * b + t - 1 if t >= 2 else TILES * b))
                    for h in range(HEADS):
                        last = act.activation(logits[s][:, h, :], logits[s][:, h, :], ACT.Exp,
                                              bias=aneg[:, 4 * s + h:4 * s + h + 1],
                                              accum_out=aden[:, 4 * s + h:4 * s + h + 1])
                    last.then_inc(exp_done, 1)

                def keep_values(t):
                    act.wait_ge(v_turned, ONE + TILES * b + t + 1)
                    act.wait_ge(pv_mm, ONE + TILES * b + (t - 1 if t >= 2 else 0))
                    act.copy(v_win[0:120, t % 2, 0:2, :].rearrange("p c n -> p (c n)"), bank[6][0:120, 0:2 * C])
                    act.copy(v_win[0:40, t % 2, 2, :], bank[6][0:40, 2 * C:3 * C]).then_inc(v_kept, 1)

                def keep_probs(t):
                    act.wait_ge(p_turned, ONE + 3 * TILES * b + 3 * t + 3)
                    act.copy(probsT[0:40, t % 2, 2, :], bank[5][0:40, 0:CH]).then_inc(p_kept_a, 1)

                def keep_out(t):
                    r0, c0 = t // (W // QC) * QR, t % (W // QC) * QC
                    act.wait_ge(pv_mm, ONE + TILES * b + t + 1)
                    act.copy(N[:, :].rearrange("p (b h w) -> p b h w", b=B, h=H)[:, ds(b, 1), r0:r0 + QR, c0:c0 + QC],
                             bank[7][:, 0:TP].rearrange("p (b h w) -> p b h w", b=1, h=QR)
                             ).then_inc(o_kept, 1)

                exps(0)
                for t in range(TILES):
                    keep_values(t)
                    if t + 1 < TILES:
                        exps(t + 1)
                    if t:
                        keep_out(t - 1)
                    keep_probs(t)
                keep_out(TILES - 1)

            norm(1, 1)
            act.wait_ge(ln_out, ONE + 2 * NCH)
            with act.Fori(0, B) as b:
                def part(g):
                    k, n = (2, C) if g < UG else (1, TAIL)
                    act.wait_ge(u_turned, ONE + 7 * b + (g - 1 if g >= 2 else 0))
                    backwards = bass.AP(S1, g % 2 * 512 + n - 1, [[4 * CH, C], [2 * n, k], [n, 2], [-1, n]])
                    act.copy(backwards, N[:, ds(b * T + g * 4 * C, 2 * k * n)].rearrange("p (n i q) -> p n q i", n=k, q=2)
                             ).then_inc(u_parted, 1)

                def high(g):
                    n, w = (C, 512) if g < UG else (TAIL, 256)
                    act.wait_ge(u_turned, ONE + 7 * b + g + 1)
                    act.activation(u16[0:n, 0, ds(b, 1)].rearrange("p b n q d -> p (b n q d)")[:, g * 512:g * 512 + w],
                                   bank[4 + g % 4][0:n, 0:w], ACT.Copy, scale=U_SCALE).then_inc(u_hi, 1)

                part(0)
                for g in range(7):
                    if g < 6:
                        part(g + 1)
                    high(g)
            with act.Fori(0, K * B) as it8:
                it = 8 * it8
                for g in range(8):
                    act.wait_ge(conv_mm, it + g + 1)
                    act.wait_ge(mix_mm, ONE + (it + g - 1 if g >= 2 else it))
                    act.copy(zs[:, g % 2, 0, :], bank[2 * (g % 2)][:, 0:CC])
                    act.copy(zs[:, g % 2, 1, :], bank[2 * (g % 2) + 1][:, 0:CC]).then_inc(z_kept, 1)

            norm(2, 0)
            norm(3, 1)
            with act.Fori(0, B) as b:
                for r in range(CPI):
                    act.wait_ge(wx_mm, CPI * b + r + 1)
                    act.copy(wx[:, r * CH:(r + 1) * CH, ds(b, 1)],
                             bank[r][:, 0:CH].unsqueeze(2)).then_inc(wx_kept, 1)

            act.wait_ge(bn_step, 1)
            act.activation(bn[:, 2:3], bn[:, 1:2], ACT.Sqrt, bias=eps[:, 1:2]).then_inc(bn_step, 1)

            def steps(n, s):
                if not (isinstance(n, int) and n == 0):
                    act.wait_ge(res_added, ONE + n - 1)
                for t in range(SB):
                    act.wait_ge(step_mm, n * SB + t + 1)
                    act.activation(ys[:, s, B * t:B * t + B], bank[s][:, B * t:B * t + B],
                                   ACT.Sigmoid).then_inc(y_ready, 1)

            steps(0, 0)
            with act.Fori(0, (NSB - 2) // 2) as n2:
                steps(2 * n2 + 1, 1)
                steps(2 * n2 + 2, 0)
            steps(NSB - 1, 1)

        @block.vector
        def _(dve):
            for signal in (ln_diff, ln_rstd, ln_out, attn_added, p_kept_v, ar_added, u_lo, mix_added, wx_stats, rec_done, res_kept):
                dve.sem_inc(signal, ONE)
            count = [0]

            def link(ins):
                count[0] += 1
                ins.then_inc(dve_set, 1)
                dve.wait_ge(dve_set, count[0])

            dve.wait_ge(c_loaded, 16 * 9)
            link(dve.tensor_tensor(small[:, 8:12], small[:, 0:4], small[:, 4:8], ALU.add))
            link(dve.tensor_reduce(small[:, 12:13], small[:, 8:12], AX.X, ALU.max))
            link(dve.tensor_scalar(small[:, 16:20], small[:, 8:12], small[:, 12:13], None, ALU.subtract))
            for n in range(3):
                k = 4 if n < 2 else 1
                dve.wait_ge(w_turned, n + 1)
                dve.tensor_copy(WT[:, 4 * n:4 * n + k, :].rearrange("p n c -> p (n c)"),
                                bank[n][:, 0:k * C]).then_inc(w_kept, 1)
            for g in range(CPI):
                dve.wait_ge(phi_turned, g + 1)
                dve.tensor_copy(phiT[:, g * CH:(g + 1) * CH], bank[3 + g % 4][0:K, 0:CH]).then_inc(phi_kept, 1)
            dve.wait_ge(phi_kept, CPI)
            link(dve.memset(taps[:, :, :, 0:C], 0.0))
            link(dve.tensor_reduce(ker[:, 1:2], phiT, AX.X, ALU.max, apply_absolute_value=True))
            link(dve.tensor_scalar(ker[:, 2:3], ker[:, 1:2], 1e-30, None, ALU.max))
            link(dve.reciprocal(ker[:, 3:4], ker[:, 2:3]))
            link(dve.tensor_scalar(ker[:, 4:5], ker[:, 3:4], PHI_SCALE, None, ALU.mult))
            for q in range(2):
                link(dve.tensor_scalar(taps[:, 0, q, C:], phiT[:, q::2], ker[:, 4:5], None, ALU.mult))
            for q in range(2):
                last = dve.scalar_tensor_tensor(out=taps[:, 1, q, C:], in0=phiT[:, q::2], scalar=ker[:, 4:5],
                                                in1=taps[:, 0, q, C:], op0=ALU.mult, op1=ALU.subtract)
            last.then_inc(taps_split, 1)
            dve.wait_ge(root_set, 2)
            link(dve.tensor_scalar(ker[:, 6:7], ker[:, 2:3], 1.0 / (PHI_SCALE * U_SCALE), None, ALU.mult))
            link(dve.tensor_tensor(ker[:, 7:8], ker[:, 5:6], ker[:, 6:7], ALU.mult))
            dve.wait_ge(consts, 1)
            dve.tensor_scalar(diag16[:, :], ident[0:K, 0:K], ker[:, 7:8], None, ALU.mult).then_inc(diag_set, 1)
            for b in range(B):
                for g in range(1, CPI, 2):
                    dve.wait_ge(x_turned, 7 * b + g + 1)
                    dve.tensor_copy(X[:, b * T + g * CH:b * T + (g + 1) * CH], bank[g][:, 0:CH]).then_inc(x_kept_v, 1)
            dve.wait_ge(sk_spread, 1)
            link(dve.tensor_copy(sk[:, :], bank[7][:, 0:K]))
            dve.wait_ge(exp_set, 1)
            link(dve.tensor_reduce(small[:, 24:25], small[:, 20:24], AX.X, ALU.add))
            link(dve.reciprocal(small[:, 25:26], small[:, 24:25]))
            link(dve.tensor_scalar(small[:, 28:32], small[:, 20:24], small[:, 25:26], None, ALU.mult))
            link(dve.tensor_reduce(small[:, 32:33], small[:, 28:32], AX.X, ALU.max))
            link(dve.tensor_scalar(small[:, 36:40], small[:, 28:32], small[:, 32:33], None, ALU.is_equal))
            link(dve.tensor_scalar(small[:, 40:44], small[:, 36:40], -1.0, 1.0, ALU.mult, ALU.add))
            link(dve.memset(small[:, 44:45], 1.0))
            for i in range(1, EXPERTS):
                link(dve.tensor_tensor(small[:, 44 + i:45 + i], small[:, 43 + i:44 + i], small[:, 39 + i:40 + i], ALU.mult))
            link(dve.tensor_tensor(small[:, 48:52], small[:, 36:40], small[:, 44:48], ALU.mult))
            link(dve.tensor_tensor(small[:, 52:56], small[:, 48:52], small[:, 28:32], ALU.subtract))
            link(dve.tensor_tensor(small[:, 56:60], small[:, 52:56], small[:, 28:32], ALU.add))
            for i in range(EXPERTS):
                dve.tensor_scalar(wsk[:, i, :], sk[:, :], small[:, 56 + i:57 + i], None, ALU.mult)
            dve.wait_ge(mu_loaded, 16)
            link(dve.tensor_scalar(Mu_eff[:, 0], mu_raw[:, 0], small[:, 56:57], None, ALU.mult))
            for i in range(1, EXPERTS):
                link(dve.scalar_tensor_tensor(out=Mu_eff[:, i], in0=mu_raw[:, i], scalar=small[:, 56 + i:57 + i],
                                              in1=Mu_eff[:, i - 1], op0=ALU.mult, op1=ALU.add))
            dve.memset(bn[:, 7:8], 0.0).then_inc(gates, 1)

            def norm(ln):
                def centre(i):
                    for u in range(4):
                        n = 4 * i + u
                        dve.wait_ge(ln_mean, ln * NCH + n + 1)
                        dve.tensor_tensor(N[:, ds(n * CH, CH)], X[:, ds(n * CH, CH)], bank[u][:, 0:CH],
                                          ALU.subtract).then_inc(ln_diff, 1)

                def invert(i):
                    dve.wait_ge(ln_std, ln * NCH // 4 + i + 1)
                    dve.reciprocal(S2[:, 1, :], S2[:, 0, :]).then_inc(ln_rstd, 1)

                def scale(i):
                    for u in range(4):
                        n = 4 * i + u
                        dve.wait_ge(ln_spread, ln * NCH + n + 1)
                        dve.tensor_tensor(N[:, ds(n * CH, CH)], N[:, ds(n * CH, CH)], bank[5 + u % 3][:, 0:CH],
                                          ALU.mult).then_inc(ln_out, 1)

                centre(0)
                with dve.Fori(0, NCH // 4 - 1) as i:
                    invert(i)
                    centre(i + 1)
                    scale(i)
                invert(NCH // 4 - 1)
                scale(NCH // 4 - 1)

            dve.wait_ge(taps_stored, 16)
            norm(0)

            dve.wait_ge(pads_set, 1)
            dve.wait_ge(bias_loaded, 16 * HEADS * QR)
            with dve.Fori(0, B) as b:
                dve.wait_ge(qk_mm, ONE + 4 * TILES * b)
                dve.wait_ge(v_turned, ONE + TILES * b)
                for c in range(CPI):
                    dve.wait_ge(qkv_mm, 21 * b + 3 * c + 1)
                    dve.tensor_scalar(qT[:, 4 * c:4 * c + 4, :].rearrange("p t (i j) -> p i t j", i=QR),
                                      bank[c % 2][:, 0:CH].rearrange("p (i t j) -> p i t j", i=QR, t=4),
                                      qkvb[:, 0:1], SCALE, ALU.add, ALU.mult).then_inc(qv_kept, 1)
                    dve.wait_ge(qkv_mm, 21 * b + 3 * c + 3)
                    dve.tensor_scalar(vpad[:, PAD + 8 * c:PAD + 8 * c + 8, PAD:PAD + W],
                                      bank[4 + c % 2][:, 0:CH].rearrange("p (h w) -> p h w", w=W),
                                      qkvb[:, 2:3], None, ALU.add).then_inc(qv_kept, 1)

                def row_max(t):
                    s = t % 2
                    dve.wait_ge(p_turned, ONE + 3 * TILES * b + (3 * t - 3 if t >= 2 else 0))
                    for h in range(HEADS):
                        dve.wait_ge(qk_mm, ONE + 4 * TILES * b + 4 * t + h + 1)
                        dve.memset(waited[:, h:h + 1], 0.0)
                        dve.tensor_tensor_reduce(out=logits[s][:, h, :], in0=bank[(HEADS * t + h) % 3][0:TP, 0:NK], in1=wbias[:, h, :],
                                                 scale=1.0, scalar=-3.0e38, op0=ALU.add, op1=ALU.max,
                                                 accum_out=amax[:, 4 * s + h:4 * s + h + 1]).then_inc(biased, 1)
                    dve.wait_ge(biased, 4 * TILES * b + 4 * t + 4)
                    dve.tensor_scalar(aneg[:, 4 * s:4 * s + 4], amax[:, 4 * s:4 * s + 4], -1.0, None,
                                      ALU.mult).then_inc(max_ready, 1)

                row_max(0)
                for t in range(TILES):
                    s = t % 2
                    dve.wait_ge(exp_done, TILES * b + t + 1)
                    dve.reciprocal(arec, aden[:, 4 * s:4 * s + 4]).then_inc(rec_done, 1)
                    dve.wait_ge(rec_done, ONE + TILES * b + t + 1)
                    dve.tensor_tensor(diag[:, s], ident[0:TP, 0:TP].unsqueeze(1).broadcast_to([TP, HEADS, TP]),
                                      arec.unsqueeze(2).broadcast_to([TP, HEADS, TP]), ALU.mult).then_inc(diag_ready, 1)
                    if t + 1 < TILES:
                        row_max(t + 1)
                    dve.wait_ge(pv_mm, ONE + TILES * b + (t - 1 if t >= 2 else 0))
                    for c in range(2):
                        dve.wait_ge(p_turned, ONE + 3 * TILES * b + 3 * t + c + 1)
                        dve.tensor_copy(probsT[0:120, s, c, :], bank[3 + c][0:120, 0:CH]).then_inc(p_kept_v, 1)
                for c in range(CPI):
                    dve.wait_ge(proj_mm, CPI * b + c + 1)
                    xs = X[:, ds(b * T + c * CH, CH)]
                    dve.scalar_tensor_tensor(out=xs, in0=bank[4 + c % 2][:, 0:CH], scalar=projb[:, 0:1], in1=xs,
                                             op0=ALU.add, op1=ALU.add).then_inc(attn_added, 1)

            norm(1)
            with dve.Fori(0, B) as b:
                for s in range(8):
                    dve.wait_ge(ar_mm, 8 * b + s + 1)
                    xs = X[:, ds(b * T + s * CC, CC)]
                    dve.tensor_tensor(xs, xs, bank[s % 4][:, 0:CC], ALU.add).then_inc(ar_added, 1)
            with dve.Fori(0, B) as b:
                for g in range(UG + 1):
                    n, w = (C, 512) if g < UG else (TAIL, 256)
                    dve.wait_ge(u_hi, 7 * b + g + 1)
                    hi, lo = (u16[0:n, h, ds(b, 1)].rearrange("p b n q d -> p (b n q d)")[:, g * 512:g * 512 + w]
                              for h in range(2))
                    dve.scalar_tensor_tensor(out=lo, in0=bank[4 + g % 4][0:n, 0:w], scalar=U_SCALE, in1=hi,
                                             op0=ALU.mult, op1=ALU.subtract).then_inc(u_lo, 1)
            with dve.Fori(0, K) as k:
                with dve.Fori(0, B) as b:
                    it = 8 * (B * k + b)
                    for g in range(8):
                        p, c = divmod(g, GPP)
                        dve.wait_ge(mix_mm, ONE + it + g + 1)
                        xs = X[:, :].rearrange("p (b t q) -> p b t q", b=B, q=2)[:, ds(b, 1), c * CC:(c + 1) * CC, p]
                        dve.tensor_tensor(xs, xs, bank[4 + g % 2][:, 0:CC].unsqueeze(1),
                                          ALU.add).then_inc(mix_added, 1)

            norm(2)
            dve.wait_ge(ln_out, ONE + 3 * NCH)
            grid = N[:, :].rearrange("p (b h w) -> p b h w", b=B, h=H)
            for b in range(B):
                dve.tensor_reduce(sums[:, 0, b, :], grid[:, b], AX.X, ALU.add).then_inc(sums_done, 1)
                dve.tensor_reduce(sums[:, 1, b, :], grid[:, b].rearrange("p h w -> p w h"), AX.X,
                                  ALU.add).then_inc(sums_done, 1)
            with dve.Fori(0, B) as b:
                for r in range(CPI):
                    dve.wait_ge(msg_mm, CPI * b + r + 1)
                    xs = X[:, ds(b * T + r * CH, CH)]
                    dve.tensor_tensor(xs, xs, bank[r][:, 0:CH], ALU.add).then_inc(msg_added, 1)

            norm(3)
            with dve.Fori(0, B) as b:
                for r in range(CPI):
                    dve.wait_ge(wx_kept, ONE + CPI * b + r + 1)
                    dve.bn_stats(stats[:, ds(CPI * b + r, 1), :], bank[r][:, 0:CH]).then_inc(wx_stats, 1)
            dve.wait_ge(wx_stats, ONE + NCH)
            dve.bn_aggr(bn[:, 0:2], stats[:, :, :].rearrange("p n s -> p (n s)")).then_inc(bn_step, 1)
            dve.wait_ge(bn_step, 2)
            link(dve.reciprocal(bn[:, 6:7], bn[:, 2:3]))
            link(dve.tensor_tensor(bn[:, 3:4], gb[:, 0:1], bn[:, 6:7], ALU.mult))
            link(dve.tensor_tensor(bn[:, 4:5], bn[:, 0:1], bn[:, 3:4], ALU.mult))
            link(dve.tensor_tensor(bn[:, 5:6], gb[:, 1:2], bn[:, 4:5], ALU.subtract))
            link(dve.memset(ys[:, 1, CH - B:CH], 0.0))
            dve.wait_ge(wx_kept, ONE + NCH)

            def scaled(n, s):
                dve.tensor_scalar(wxn[:, s, :].rearrange("p (t b) -> p t b", b=B), wx[:, ds(n * SB, SB), :],
                                  bn[:, 3:4], bn[:, 5:6], ALU.mult, ALU.add).then_inc(wx_normed, 1)

            def keep(m, s):
                dve.wait_ge(res_turned, ONE + m + 1)
                if not (isinstance(m, int) and m < 2):
                    dve.wait_ge(stored[s], 8 * (m - s))
                dve.tensor_copy(o_out[:, s].rearrange("p b c -> p (b c)"), bank[4 + s][0:SB, :]).then_inc(res_kept, 1)

            scaled(0, 0)
            scaled(1, 1)
            for n in range(2):
                dve.wait_ge(wx_placed, n + 1)
                scaled(n + 2, n)
                keep(n, n)
            with dve.Fori(1, (NSB - 2) // 2) as n2:
                for s in range(2):
                    n = 2 * n2 + s
                    dve.wait_ge(wx_placed, n + 1)
                    scaled(n + 2, s)
                    keep(n, s)
            keep(NSB - 2, 0)
            keep(NSB - 1, 1)


_INS = ["x", "L0_conv_qkv_w", "L0_conv_qkv_b", "L0_conv_rpb", "L0_conv_proj_w", "L0_conv_proj_b", "L0_ffn_sigma",
        "L0_ffn_phi", "L0_ffn_M_u", "L0_ffn_M_phi_plus", "L0_ffn_M_phi_minus", "L0_ffn_log_weights", "L0_ffn_gumbel",
        "L1_conv_Wself", "L1_conv_Wm", "L1_conv_Wk", "L1_ffn_W", "L1_ffn_V", "L1_ffn_gamma", "L1_ffn_beta"]


def kernel(**inputs):
    import numpy as _np
    import concourse.bacc as _bacc
    from concourse import mybir as _mybir
    from concourse.bass_utils import run_bass_kernel_spmd as _run

    nc = _bacc.Bacc("TRN2", target_bir_lowering=False, num_devices=1)
    arrays, args = {}, []
    for name in _INS:
        a = _np.ascontiguousarray(inputs[name])
        arrays[f"in_{name}_dram"] = a
        args.append(nc.dram_tensor(f"in_{name}_dram", a.shape, _mybir.dt.from_np(a.dtype), kind="ExternalInput").ap())
    args.append(nc.dram_tensor("out_0_dram", (B, H, W, C), F32, kind="ExternalOutput").ap())
    build(nc, *args)
    r = _run(nc, [arrays], core_ids=[0])
    return r.results[0]["out_0_dram"]
```

```python
from contextlib import ExitStack

import concourse.bass as bass
from concourse import mybir

ALU = mybir.AluOpType
ACT = mybir.ActivationFunctionType
AX = mybir.AxisListType
F32 = mybir.dt.float32
F16 = mybir.dt.float16
ds = bass.ds

C = 128
B, H, W = 4, 56, 56
T = H * W
NT = B * T
CH = 448
NCH = NT // CH
CPI = T // CH
TP = 112
TPI = T // TP

XA, XV = 4 * B, 3 * B

HEADS, HD, KS, PAD = 4, 32, 7, 3
SCALE = HD ** -0.5
QR, QC = 8, 14
KR, KC = QR + KS - 1, QC + KS - 1
NK = KR * KC
HP, WP = H + 2 * PAD, W + 2 * PAD
TILES = (H // QR) * (W // QC)
KEY_CHUNKS = [(0, 6), (6, 6), (12, 2)]
ER, EC = QR + KR - 1, QC + KC - 1
OUTSIDE = -1.0e30

K, L = 16, T // 2
NB = -(-L // C)
TAIL = L - (NB - 1) * C
UG = T // (4 * C)
PAIRS = NB // 2
PH = PAIRS // 2
CU = PH * C
SPAN = 4 * CU
CC = 392
TAPW = C + L
TW = [L + 1, 2 * PAIRS * C + 1]
EXPERTS, AR = 4, 3
U_SCALE, PHI_SCALE = 256.0, 1024.0
EIGHTHS = [3, 2, 1, 1, 0, 0, 0, 0]


def unit_of(g):
    return g // 2, 1 - g % 2


def reach_spans(h, a):
    def reach(col):
        token = (2 * (PH * h + col // C) + a) * C + col % C
        return sum(token < (L >> i) for i in range(1, EXPERTS))
    edges = [c for c in range(CU) if c == 0 or reach(c) != reach(c - 1)] + [CU]
    return [(lo, hi, reach(lo)) for lo, hi in zip(edges, edges[1:])]


SPANS = [reach_spans(h, a) for h in range(2) for a in range(2)]

ONE = 1

SB = 112
NSB = T // SB


def build(nc, x, qkv_w, qkv_b, rpb, proj_w, proj_b, sigma, phi, M_u, M_plus, M_minus, log_w, gumbel,
          Wself, Wm, Wk, Wr, Vr, gamma, beta, out):
    with ExitStack() as ctx:
        def sb(name, shape, dt=F32):
            return ctx.enter_context(nc.sbuf_tensor(name, shape, dt))

        def sem(name):
            return ctx.enter_context(nc.semaphore(name))

        bank = [ctx.enter_context(nc.psum_tensor(f"bank{i}", [C, 512], F32)) for i in range(8)]

        X = sb("X", [C, NT])
        N = sb("N", [C, NT])
        A = sb("A", [C, 14336])
        WT = sb("WT", [C, 9, C])
        ident = sb("ident", [C, C])
        mean_w = sb("mean_w", [C, C])
        spread_w = sb("spread_w", [C, 4, C])
        ones16 = sb("ones16", [K, C])
        qkvb = sb("qkvb", [C, 3])
        projb = sb("projb", [C, 1])
        gb = sb("gb", [C, 2])
        SIDE_W = 6 * CH + EXPERTS * AR * C
        SIDE = sb("SIDE", [C, SIDE_W])
        S1 = SIDE[:, 0:4 * CH].rearrange("p (s n) -> p s n", s=4)
        S2 = SIDE[:, 4 * CH:6 * CH].rearrange("p (s n) -> p s n", s=2)
        Mu_eff = SIDE[:, 6 * CH:].rearrange("p (i a e) -> p i a e", i=EXPERTS, a=AR)
        small = sb("small", [C, 64])
        wsk = sb("wsk", [C, EXPERTS, K])
        sk = sb("sk", [C, K])
        ker = sb("ker", [K, 8])
        diag16 = sb("diag16", [K, K])
        sums = sb("sums", [C, 2, B, H])
        stats = sb("stats", [C, NCH, 6])
        bn = sb("bn", [C, 8])
        unit = sb("unit", [C, 1])
        eps = sb("eps", [C, 2])
        WORK = sb("WORK", [C, 6144])

        x_tok = A[0:TP, :].rearrange("p (b j c) -> p b j c", b=B, c=C)
        w_raw = N[:, 0:9 * C].rearrange("p (n c) -> p n c", c=C)
        phi_raw = N[0:TP, 2048:2048 + TPI * K].rearrange("p (j k) -> p j k", k=K)
        mu_raw = N[:, 4096:4096 + EXPERTS * AR * C].rearrange("p (i a e) -> p i a e", i=EXPERTS, a=AR)
        phiT = N[0:K, 5760:5760 + T]
        taps = N[0:K, 9152:9152 + 2 * TAPW].bitcast(F16).rearrange("p (h q w) -> p h q w", h=2, q=2)
        diff_raw = WORK[0:K, 0:L]
        diffs = WORK[0:K, L:L + 2 * TAPW].bitcast(F16).rearrange("p (h q w) -> p h q w", h=2, q=2)
        window = WORK[0:HEADS, 6144 - ER * EC:6144].rearrange("p (a b) -> p a b", a=ER)
        kpad = A[:, 0:HP * WP].rearrange("p (h w) -> p h w", h=HP)
        vpad = A[:, HP * WP:2 * HP * WP].rearrange("p (h w) -> p h w", h=HP)
        qT = A[:, 2 * HP * WP:2 * HP * WP + T].rearrange("p (t n) -> p t n", t=TILES)
        wbias = A[0:TP, 10880:10880 + HEADS * NK].rearrange("p (h k) -> p h k", h=HEADS)
        logits = [A[0:TP, 12032:12032 + HEADS * NK].rearrange("p (h k) -> p h k", h=HEADS),
                  WORK[0:TP, 0:HEADS * NK].rearrange("p (h k) -> p h k", h=HEADS)]
        probsT = WORK[:, 1152:1152 + 6 * CH].rearrange("p (s c n) -> p s c n", s=2, c=3)
        v_win = WORK[:, 3840:3840 + 6 * C].rearrange("p (s c n) -> p s c n", s=2, c=3)
        amax = WORK[0:TP, 4608:4616]
        aneg = WORK[0:TP, 4616:4624]
        aden = WORK[0:TP, 4624:4632]
        arec = WORK[0:TP, 4632:4636]
        waited = WORK[0:TP, 4636:4640]
        v_chan = WORK[:, 4640:4640 + 2 * NK].rearrange("p (s k) -> p s k", s=2)
        diag = WORK[0:TP, 5200:5200 + 2 * CH].rearrange("p (s h q) -> p s h q", s=2, h=HEADS)
        u16 = A[:, 0:B * NB * 2 * C].bitcast(F16).rearrange("p (h b n q d) -> p h b n q d", h=2, b=B, q=2, n=NB)
        u_part = SIDE[:, 0:1024].rearrange("p (s n) -> p s n", s=2)
        u_sum = S2[:, :, 0:2 * C]
        x16 = WORK[:, :].bitcast(F16).rearrange("p (h b j q d) -> p h b j q d", h=2, b=B, q=2, j=PAIRS)
        N16 = N[:, :].bitcast(F16)
        toep = [N16[:, h * 4 * TW[0]:(h + 1) * 4 * TW[0]].rearrange("p (h q w) -> p h q w", h=2, q=2)
                for h in range(2)]
        toep_end = 8 * TW[0]
        diff = [N16[:, toep_end + h * 4 * TW[1]:toep_end + (h + 1) * 4 * TW[1]]
                .rearrange("p (h q w) -> p h q w", h=2, q=2) for h in range(2)]
        m_raw = A[:, B * NB * 2 * C:B * NB * 2 * C + 1024].rearrange("p (s i e) -> p s i e", s=2, i=EXPERTS)
        m_eff = [SIDE[:, h * 1024:(h + 1) * 1024].rearrange("p (s i e) -> p s i e", s=2, i=EXPERTS) for h in range(2)]
        m_sum = SIDE[:, 2048:2560].rearrange("p (i e) -> p i e", i=EXPERTS)
        zs = SIDE[:, 2560:2560 + 4 * CU].rearrange("p (e a n) -> p e a n", e=2, a=2)
        z_tail = SIDE[:, 2560 + 4 * CU:2560 + 4 * CU + 4 * TAIL].rearrange("p (e n) -> p e n", e=2)
        lines = SIDE[:, 0:B * (H + W)].rearrange("p (b n) -> p b n", b=B)
        wx = A[:, 0:NT].rearrange("p (t b) -> p t b", b=B)
        wxn = WORK[:, 0:2 * CH].rearrange("p (s n) -> p s n", s=2)
        ys = WORK[:, 896:896 + 2 * CH].rearrange("p (s n) -> p s n", s=2)
        res = WORK[:, 1792:1792 + 2 * CH].rearrange("p (s n) -> p s n", s=2)
        o_out = WORK[0:TP, 2688:2688 + 1024].rearrange("p (s b c) -> p s b c", s=2, b=B)

        WQ, WKEY, WV, WP_, WSELF, WM, WK_, WR, WV_R = range(9)

        window_d = nc.dram_tensor("window_d", [HEADS, TP, ER * EC], F32)
        taps_d = nc.dram_tensor("taps_d", [K * 4 * TAPW], F16)
        diffs_d = nc.dram_tensor("diffs_d", [K * 4 * TAPW], F16)

        w_loaded = sem("w_loaded"); c_loaded = sem("c_loaded"); x_loaded = [sem(f"x_loaded{b}") for b in range(B)]
        phi_loaded = sem("phi_loaded"); mu_loaded = sem("mu_loaded")
        rpb_loaded = sem("rpb_loaded"); window_stored = sem("window_stored"); bias_loaded = sem("bias_loaded")
        taps_stored = sem("taps_stored"); diffs_split = sem("diffs_split")
        pool_set = sem("pool_set"); spread_set = sem("spread_set"); consts = sem("consts"); window_set = sem("window_set"); pads_set = sem("pads_set")
        w_turned = sem("w_turned"); w_kept = sem("w_kept")
        phi_turned = sem("phi_turned"); phi_kept = sem("phi_kept")
        taps_split = sem("taps_split"); dve_set = sem("dve_set"); exp_set = sem("exp_set")
        sk_spread = sem("sk_spread"); gates = sem("gates"); diag_set = sem("diag_set")
        x_turned = sem("x_turned"); x_kept_a = sem("x_kept_a"); x_kept_v = sem("x_kept_v")
        ln_mean = sem("ln_mean"); ln_diff = sem("ln_diff"); ln_sq = sem("ln_sq")
        root_set = sem("root_set"); ln_var = sem("ln_var"); ln_std = sem("ln_std"); ln_rstd = sem("ln_rstd"); ln_spread = sem("ln_spread"); ln_out = sem("ln_out")
        qkv_mm = sem("qkv_mm"); qv_kept = sem("qv_kept"); k_kept = sem("k_kept")
        qk_mm = sem("qk_mm"); biased = sem("biased"); max_ready = sem("max_ready"); exp_done = sem("exp_done")
        v_cut = sem("v_cut"); v_turned = sem("v_turned"); v_kept = sem("v_kept")
        p_turned = sem("p_turned"); p_kept_v = sem("p_kept_v"); p_kept_a = sem("p_kept_a")
        pv_mm = sem("pv_mm"); rec_done = sem("rec_done"); diag_ready = sem("diag_ready")
        o_kept = sem("o_kept"); proj_mm = sem("proj_mm"); attn_added = sem("attn_added")
        ar_mm = sem("ar_mm"); ar_added = sem("ar_added")
        u_parted = sem("u_parted"); u_turned = sem("u_turned"); u_hi = sem("u_hi"); u_lo = sem("u_lo")
        u_first = sem("u_first"); u_summed = sem("u_summed"); x_hi = sem("x_hi"); x_lo = sem("x_lo")
        toep_loaded = [sem("toep_loaded0"), sem("toep_loaded1")]
        m_loaded = sem("m_loaded")
        m_summed = sem("m_summed"); m_step = sem("m_step"); m_ready = sem("m_ready")
        conv_mm = sem("conv_mm"); z_shared = sem("z_shared"); z_kept = sem("z_kept"); mix_mm = sem("mix_mm"); mix_added = sem("mix_added")
        sums_done = sem("sums_done"); msg_mm = sem("msg_mm"); msg_added = sem("msg_added")
        lines_mm = sem("lines_mm"); lines_kept = sem("lines_kept"); lines_spread = sem("lines_spread")
        lines_added = sem("lines_added")
        wx_mm = sem("wx_mm"); wx_stats = sem("wx_stats"); wx_kept = sem("wx_kept"); bn_step = sem("bn_step")
        wx_normed = sem("wx_normed"); wx_placed = sem("wx_placed")
        step_mm = sem("step_mm"); y_ready = sem("y_ready")
        res_added = sem("res_added"); res_turned = sem("res_turned"); res_kept = sem("res_kept")
        stored = [sem("stored0"), sem("stored1")]

        x_d = x.rearrange("b h w c -> b (h w) c").rearrange("b (j p) c -> b p j c", p=TP)
        out_d = out.rearrange("b h w c -> b (h w) c").rearrange("b t c -> t b c")

        block = ctx.enter_context(nc.Block())

        @block.sync
        def _(sp):
            for n, w in enumerate([qkv_w[0:C, :], qkv_w[C:2 * C, :], qkv_w[2 * C:3 * C, :], proj_w,
                                   Wself, Wm, Wk, Wr, Vr]):
                sp.dma_start(w_raw[:, n, :], w).then_inc(w_loaded, 16)
            for b in range(B):
                sp.dma_start(x_tok[:, b], x_d[b]).then_inc(x_loaded[b], 16)
            sp.wait_ge(window_set, 1)
            for h in range(HEADS):
                sp.dma_start(window[h:h + 1, QR - 1:QR - 1 + KS, QC - 1:QC - 1 + KS],
                             rpb[h:h + 1, PAD:PAD + KS, PAD:PAD + KS]).then_inc(rpb_loaded, 16)
            sp.wait_ge(rpb_loaded, 16 * HEADS)
            sp.dma_start(window_d.ap(), window.rearrange("p a b -> p (a b)").unsqueeze(1)
                         .broadcast_to([HEADS, TP, ER * EC])).then_inc(window_stored, 16)
            sp.wait_ge(taps_split, 1)
            sp.dma_start(taps_d.ap().rearrange("(k n) -> k n", k=K),
                         taps.rearrange("p h q w -> p (h q w)")).then_inc(taps_stored, 16)
            sp.wait_ge(diffs_split, 2)
            sp.dma_start(diffs_d.ap().rearrange("(k n) -> k n", k=K),
                         diffs.rearrange("p h q w -> p (h q w)")).then_inc(taps_stored, 16)
            sp.wait_ge(window_stored, 16)
            sp.wait_ge(x_kept_a, XA)
            sp.wait_ge(x_kept_v, XV)
            for h in range(HEADS):
                for qi in range(QR):
                    src = bass.AP(window_d, (h * TP + qi * QC) * ER * EC + (QR - 1 - qi) * EC + QC - 1,
                                  [[ER * EC - 1, QC], [EC, KR], [1, KC]])
                    sp.dma_start(wbias[qi * QC:(qi + 1) * QC, h, :].rearrange("p (a b) -> p a b", a=KR),
                                 src).then_inc(bias_loaded, 16)
            sp.wait_ge(attn_added, ONE + NCH)
            sp.wait_ge(ar_mm, B * 8)
            sp.wait_ge(u_turned, ONE + B * 7)
            sp.wait_ge(taps_stored, 32)
            for k in range(K):
                half = k % 2
                if k >= 2:
                    sp.wait_ge(mix_mm, ONE + 4 * B * (k - 1))
                for blocks, taps_of, width in ((toep, taps_d, TW[0]), (diff, diffs_d, TW[1])):
                    src = bass.AP(taps_of, k * 4 * TAPW, [[1, C], [TAPW, 4], [1, width]])
                    sp.dma_start(blocks[half].rearrange("p h q w -> p (h q) w"), src).then_inc(toep_loaded[half], 16)
                if k:
                    sp.wait_ge(m_step, 3 * k - 2)
                for s, m in enumerate((M_plus, M_minus)):
                    sp.dma_start(m_raw[:, s], m[:, k].rearrange("i d e -> d i e")).then_inc(m_loaded, 16)
            with sp.Fori(0, NSB // 2) as n2:
                for s in range(2):
                    sp.wait_ge(res_kept, ONE + 2 * n2 + s + 1)
                    sp.dma_start(out_d[ds((2 * n2 + s) * SB, SB)], o_out[:, s]).then_inc(stored[s], 16)
            for s in range(2):
                sp.wait_ge(stored[s], 16 * (NSB // 2))

        @block.gpsimd
        def _(pool):
            for signal in (res_added,):
                pool.sem_inc(signal, ONE)
            pool.memset(unit[:, :], 1.0)
            pool.memset(eps[:, 0:1], 1e-6)
            pool.memset(eps[:, 1:2], 1e-5)
            pool.memset(mean_w[:, :], 1.0 / C)
            pool.memset(ones16[:, :], 1.0)
            pool.memset(ident[:, :], 0.0).then_inc(pool_set, 1)
            pool.wait_ge(pool_set, 1)
            pool.affine_select(out=ident[:, :], in_=ident[:, :], compare_op=ALU.not_equal, fill=1.0, base=0,
                               pattern=[[-1, C]], channel_multiplier=1).then_inc(consts, 1)
            pool.memset(window, OUTSIDE).then_inc(window_set, 1)
            pool.memset(spread_w[:, :, :], 0.0).then_inc(pool_set, 1)
            pool.wait_ge(pool_set, 2)
            for u in range(4):
                if u:
                    pool.wait_ge(spread_set, u)
                pool.memset(spread_w[32 * u:32 * u + 32, u, :], 1.0 / 32).then_inc(spread_set, 1)
            pool.wait_ge(spread_set, 4)
            for n in range(3):
                pool.dma_start(qkvb[:, n:n + 1], qkv_b[n * C:(n + 1) * C].rearrange("(p a) -> p a", a=1)).then_inc(c_loaded, 16)
            pool.dma_start(projb[:, :], proj_b.rearrange("(p a) -> p a", a=1)).then_inc(c_loaded, 16)
            pool.dma_start(gb[:, 0:1], gamma.rearrange("(p a) -> p a", a=1)).then_inc(c_loaded, 16)
            pool.dma_start(gb[:, 1:2], beta.rearrange("(p a) -> p a", a=1)).then_inc(c_loaded, 16)
            pool.dma_start(ker[:, 0:1], sigma.rearrange("(p a) -> p a", a=1)).then_inc(c_loaded, 16)
            pool.dma_start(small[:, 0:4], bass.AP(log_w.tensor, 0, [[0, C], [1, 4]])).then_inc(c_loaded, 16)
            pool.dma_start(small[:, 4:8], bass.AP(gumbel.tensor, 0, [[0, C], [1, 4]])).then_inc(c_loaded, 16)
            pool.dma_start(phi_raw, phi[0:T, :].rearrange("(j p) k -> p j k", p=TP)).then_inc(phi_loaded, 16)
            pool.dma_start(mu_raw, M_u.rearrange("i a d e -> d i a e")).then_inc(mu_loaded, 16)

            pool.wait_ge(x_kept_a, XA)
            pool.wait_ge(x_kept_v, XV)
            pool.memset(A[:, 0:2 * HP * WP], 0.0).then_inc(pads_set, 1)
            with pool.Fori(0, B) as b:
                pool.wait_ge(qv_kept, 14 * b + 14)
                for t in range(TILES):
                    r0, c0 = t // (W // QC) * QR, t % (W // QC) * QC
                    pool.wait_ge(v_turned, ONE + TILES * b + (t - 1 if t >= 2 else 0))
                    keys = vpad[:, r0:r0 + KR, c0:c0 + KC]
                    pool.tensor_tensor(v_chan[:, t % 2].rearrange("p (h w) -> p h w", h=KR), keys,
                                       unit[:, :].unsqueeze(2).broadcast_to([C, KR, KC]), ALU.mult).then_inc(v_cut, 1)
            pool.wait_ge(gates, 1)
            pool.wait_ge(u_turned, ONE + 7 * B)
            pool.wait_ge(ar_mm, 8 * B)
            pool.wait_ge(x_lo, ONE + 6 * B)

            def matrices(k, half):
                pool.wait_ge(m_loaded, 32 * k + 32)
                pool.tensor_tensor(m_sum[:, :], m_raw[:, 0], m_raw[:, 1], ALU.add)
                pool.tensor_tensor(m_raw[:, 0], m_raw[:, 0], m_raw[:, 1], ALU.subtract).then_inc(m_summed, 1)
                pool.wait_ge(m_summed, k + 1)
                if not isinstance(k, int):
                    pool.wait_ge(mix_mm, ONE + 4 * B * (k - 1))
                for e, source in enumerate((m_sum, m_raw[:, 0])):
                    last = pool.tensor_tensor(m_eff[half][:, e], source,
                                              wsk[:, :, ds(k, 1)].broadcast_to([C, EXPERTS, C]), ALU.mult)
                last.then_inc(m_step, 1)
                for r in range(1, EXPERTS):
                    pool.wait_ge(m_step, 3 * k + r)
                    pool.tensor_tensor(m_eff[half][:, :, r], m_eff[half][:, :, r], m_eff[half][:, :, r - 1],
                                       ALU.add).then_inc(m_step if r < EXPERTS - 1 else m_ready, 1)

            matrices(0, 0)
            matrices(1, 1)
            with pool.Fori(1, K // 2) as k2:
                for half in range(2):
                    matrices(2 * k2 + half, half)
            for b in range(B):
                pool.wait_ge(msg_mm, CPI * b + CPI)
                pool.wait_ge(lines_kept, b + 1)
                pool.tensor_tensor(N[:, b * T:(b + 1) * T].rearrange("p (h w) -> p h w", h=H),
                                   lines[:, b, 0:H].unsqueeze(2).broadcast_to([C, H, W]),
                                   lines[:, b, H:H + W].unsqueeze(1).broadcast_to([C, H, W]),
                                   ALU.add).then_inc(lines_spread, 1)
            with pool.Fori(0, NSB // 2) as n2:
                for s in range(2):
                    n = 2 * n2 + s
                    pool.wait_ge(y_ready, n * SB + SB)
                    pool.wait_ge(res_turned, ONE + n)
                    pool.tensor_tensor(res[:, s].rearrange("p (b t) -> p b t", b=B),
                                       X[:, :].rearrange("p (b t) -> p b t", b=B)[:, :, ds(n * SB, SB)],
                                       ys[:, s].rearrange("p (t b) -> p b t", b=B), ALU.add).then_inc(res_added, 1)

        @block.tensor
        def _(pe):
            for signal in (v_turned, qk_mm, p_turned, pv_mm, u_turned, mix_mm, ln_var, res_turned):
                pe.sem_inc(signal, ONE)
            pe.wait_ge(consts, 1)
            pe.wait_ge(w_loaded, 16 * 9)
            for n in range(9):
                mm = pe.transpose(bank[n // 4][:, n % 4 * C:(n % 4 + 1) * C], w_raw[:, n, :], ident[:, :])
                if n in (3, 7, 8):
                    mm.then_inc(w_turned, 1)
            pe.wait_ge(phi_loaded, 16)
            for g in range(CPI):
                if g >= 4:
                    pe.wait_ge(phi_kept, g - 3)
                for j in range(4):
                    mm = pe.transpose(bank[3 + g % 4][0:K, j * TP:(j + 1) * TP], phi_raw[:, 4 * g + j, :],
                                      ident[0:TP, 0:TP])
                mm.then_inc(phi_turned, 1)
            pe.wait_ge(w_kept, 3)
            pe.wait_ge(phi_kept, CPI)
            for b in range(B):
                pe.wait_ge(x_loaded[b], 16)
                if b:
                    pe.wait_ge(x_kept_a, 4 * b)
                    pe.wait_ge(x_kept_v, 3 * b)
                for g in range(CPI):
                    for j in range(4):
                        mm = pe.transpose(bank[g][:, j * TP:(j + 1) * TP], x_tok[:, b, 4 * g + j, :],
                                          ident[0:TP, 0:TP])
                    mm.then_inc(x_turned, 1)
            pe.wait_ge(diag_set, 1)
            pe.matmul(bank[7][:, 0:K], ones16[:, :], diag16[:, :], start=True, stop=True).then_inc(sk_spread, 1)

            def norm(ln):
                def means(i):
                    pe.wait_ge(ln_diff, ONE + ln * NCH + 4 * i)
                    for u in range(4):
                        pe.matmul(bank[u][:, 0:CH], mean_w[:, :], X[:, ds((4 * i + u) * CH, CH)],
                                  start=True, stop=True).then_inc(ln_mean, 1)

                def variances(i):
                    for u in range(4):
                        pe.wait_ge(ln_sq, ln * NCH + 4 * i + u + 1)
                        mm = pe.matmul(bank[4][32 * u:32 * u + 32, 0:CH], mean_w[:, 0:32], S1[:, u, :],
                                       start=True, stop=True)
                    mm.then_inc(ln_var, 1)

                def spread(i):
                    pe.wait_ge(ln_rstd, ONE + ln * NCH // 4 + i + 1)
                    for u in range(4):
                        if u == 3:
                            pe.wait_ge(ln_out, ONE + ln * NCH + 4 * i + 1)
                        pe.matmul(bank[5 + u % 3][:, 0:CH], spread_w[:, u, :], S2[:, 1, :], start=True, stop=True).then_inc(ln_spread, 1)

                means(0)
                with pe.Fori(0, NCH // 4 - 1) as i:
                    variances(i)
                    means(i + 1)
                    spread(i)
                variances(NCH // 4 - 1)
                spread(NCH // 4 - 1)

            pe.wait_ge(x_kept_a, XA)
            pe.wait_ge(x_kept_v, XV)
            pe.wait_ge(gates, 1)
            pe.wait_ge(spread_set, 4)
            norm(0)

            pe.wait_ge(ln_out, ONE + NCH)
            with pe.Fori(0, B) as b:
                pe.wait_ge(attn_added, ONE + CPI * b)
                for c in range(CPI):
                    for n, w in enumerate((WQ, WKEY, WV)):
                        if c >= 2 and n == 0:
                            pe.wait_ge(qv_kept, 14 * b + 2 * c - 3)
                        if c >= 2 and n == 1:
                            pe.wait_ge(k_kept, 7 * b + c - 1)
                        if c >= 2 and n == 2:
                            pe.wait_ge(qv_kept, 14 * b + 2 * c - 2)
                        pe.matmul(bank[2 * n + c % 2][:, 0:CH], WT[:, w, :], N[:, ds(b * T + c * CH, CH)],
                                  start=True, stop=True).then_inc(qkv_mm, 1)
                pe.wait_ge(qv_kept, 14 * b + 14)
                pe.wait_ge(k_kept, 7 * b + 7)

                def scores(t):
                    r0, c0 = t // (W // QC) * QR, t % (W // QC) * QC
                    for h in range(HEADS):
                        i = HEADS * t + h
                        if i >= 3:
                            pe.wait_ge(biased, 4 * TILES * b + i - 2)
                        p = slice(h * HD, (h + 1) * HD)
                        pe.matmul(bank[i % 3][0:TP, 0:NK], qT[p, t, :],
                                  kpad[p, r0:r0 + KR, c0:c0 + KC], start=True, stop=True).then_inc(qk_mm, 1)

                def turn_values(t):
                    pe.wait_ge(v_cut, TILES * b + t + 1)
                    pe.wait_ge(v_kept, ONE + TILES * b + t)
                    for c, (kr, nr) in enumerate(KEY_CHUNKS):
                        mm = pe.transpose(bank[6][0:nr * KC, c * C:(c + 1) * C],
                                          v_chan[:, t % 2, kr * KC:(kr + nr) * KC], ident[:, :])
                    mm.then_inc(v_turned, 1)

                def turn_probs(t):
                    pe.wait_ge(diag_ready, TILES * b + t + 1)
                    pe.wait_ge(p_kept_v, ONE + 2 * TILES * b + 2 * t)
                    pe.wait_ge(p_kept_a, ONE + TILES * b + t)
                    for c, (kr, nr) in enumerate(KEY_CHUNKS):
                        for h in range(HEADS):
                            mm = pe.matmul(bank[3 + c][0:nr * KC, h * TP:(h + 1) * TP],
                                           logits[t % 2][:, h, kr * KC:(kr + nr) * KC], diag[:, t % 2, h, :],
                                           start=True, stop=True)
                        mm.then_inc(p_turned, 1)

                def outputs(t):
                    pe.wait_ge(p_kept_v, ONE + 2 * TILES * b + 2 * t + 2)
                    pe.wait_ge(p_kept_a, ONE + TILES * b + t + 1)
                    pe.wait_ge(v_kept, ONE + TILES * b + t + 1)
                    pe.wait_ge(o_kept, ONE + TILES * b + t)
                    for c, (kr, nr) in enumerate(KEY_CHUNKS):
                        for h in range(HEADS):
                            mm = pe.matmul(bank[7][h * HD:(h + 1) * HD, 0:TP],
                                           v_win[0:nr * KC, t % 2, c, h * HD:(h + 1) * HD],
                                           probsT[0:nr * KC, t % 2, c, h * TP:(h + 1) * TP],
                                           start=(c == 0), stop=(c == 2), skip_group_check=True)
                    mm.then_inc(pv_mm, 1)

                scores(0)
                for t in range(TILES):
                    if t + 1 < TILES:
                        scores(t + 1)
                    turn_values(t)
                    if t:
                        outputs(t - 1)
                    turn_probs(t)
                outputs(TILES - 1)
                pe.wait_ge(o_kept, ONE + TILES * b + TILES)
                for c in range(CPI):
                    if c >= 2:
                        pe.wait_ge(attn_added, ONE + CPI * b + c - 1)
                    pe.matmul(bank[4 + c % 2][:, 0:CH], WT[:, WP_, :], N[:, ds(b * T + c * CH, CH)],
                              start=True, stop=True).then_inc(proj_mm, 1)

            pe.wait_ge(attn_added, ONE + NCH)
            norm(1)
            pe.wait_ge(ln_out, ONE + 2 * NCH)
            with pe.Fori(0, B) as b:
                pe.wait_ge(ar_added, ONE + 8 * b)
                for s, reach in enumerate(EIGHTHS):
                    if s >= 4:
                        pe.wait_ge(ar_added, ONE + 8 * b + s - 3)
                    for a in range(AR):
                        cut = a if s == 0 else 0
                        mm = pe.matmul(bank[s % 4][:, cut:CC], Mu_eff[:, reach, a, :],
                                       N[:, ds(b * T + s * CC - a + cut, CC - cut)],
                                       start=(a == 0), stop=(a == AR - 1))
                    mm.then_inc(ar_mm, 1)
                    if s < UG + 1:
                        n = C if s < UG else TAIL
                        pe.wait_ge(u_parted, 7 * b + s + 1)
                        pe.wait_ge(u_lo, ONE + 7 * b + (s - 3 if s >= 4 else 0))
                        for j in range(4 if s < UG else 2):
                            mm = pe.transpose(bank[4 + s % 4][0:n, j * C:(j + 1) * C],
                                              u_part[:, s % 2, j * n:(j + 1) * n], ident[:, :])
                        mm.then_inc(u_turned, 1)
            pe.wait_ge(x_lo, ONE + 6 * B)
            pe.wait_ge(u_lo, ONE + 7 * B)
            pe.wait_ge(ar_added, ONE + 8 * B)

            with pe.Fori(0, K // 2) as k2:
                def unit_no(half, b, g):
                    return 4 * (B * (2 * k2 + half) + b) + g

                def conv(half, b, g, e):
                    p, h = unit_of(g)
                    q, shift = p ^ e, (1 if e > p else 0)
                    last = PH * (h + 1) - 1
                    for j in range(last + 1):
                        i0 = max(j, PH * h)
                        n = last + 1 - i0
                        at = 1 - shift + 2 * (i0 - j) * C
                        for o, (left, right, w) in enumerate((
                                (x16[:, :, b, j, q, :], toep[half], at),
                                (u16[:, :, b, 2 * j + 1, q, :], diff[half], at),
                                (u16[:, :, b, 2 * j, q, :], diff[half], at + C))):
                            for x, (hu, hp) in enumerate(((0, 0), (0, 1), (1, 0))):
                                taps_in = right[:, hp, e, w:w + 2 * n * C - C]
                                if n > 1:
                                    taps_in = bass.AP(taps_in.tensor, taps_in.offset,
                                                      [list(taps_in.ap[0]), [2 * C, n], [1, C]])
                                mm = pe.matmul(bank[3 * e + o][:, (i0 - PH * h) * C:CU], left[:, hu, :], taps_in,
                                               start=(j == 0 and x == 0), stop=(j == last and x == 2))
                    return mm

                def tail(half, b):
                    for n in range(NB):
                        rows = C if n < NB - 1 else TAIL
                        at = 1 + (NB - 1 - n) * C + (C - rows)
                        for q in range(2):
                            first, step = CU + q * TAIL, (3 - 2 * q) * TAIL
                            dest = bank[0][:, first:first + step + TAIL]
                            dest = bass.AP(dest.tensor, dest.offset, [list(dest.ap[0]), [step, 2], [1, TAIL]])
                            for x, (hu, hp) in enumerate(((0, 0), (0, 1), (1, 0))):
                                taps_in = toep[half][0:rows, hp, 0, at:at + TAIL]
                                taps_in = bass.AP(taps_in.tensor, taps_in.offset,
                                                  [list(taps_in.ap[0]), [TW[0] - q, 2], [1, TAIL]])
                                mm = pe.matmul(dest, u16[0:rows, hu, b, n, q, :], taps_in,
                                               start=(n == 0 and q == 0 and x == 0),
                                               stop=(n == NB - 1 and x == 2), skip_group_check=True)
                    return mm

                def mix(half, b, g):
                    unit = unit_no(half, b, g)
                    pe.wait_ge(z_kept, ONE + 2 * unit + 2)
                    pe.wait_ge(mix_added, ONE + unit)
                    for a in range(2):
                        for lo, hi, reach in SPANS[2 * unit_of(g)[1] + a]:
                            for e in range(2):
                                mm = pe.matmul(bank[6 + a][:, lo:hi], m_eff[half][:, e, reach, :],
                                               zs[:, e, a, lo:hi], start=(e == 0), stop=(e == 1))
                    if g == 3:
                        for e in range(2):
                            mm = pe.matmul(bank[6][:, CU:CU + 2 * TAIL], m_eff[half][:, e, 0, :],
                                           z_tail[:, e, :], start=(e == 0), stop=(e == 1))
                    mm.then_inc(mix_mm, 1)

                before = None
                for half in range(2):
                    pe.wait_ge(toep_loaded[half], 32 * k2 + 32)
                    for b in range(B):
                        for g in range(4):
                            kept = ONE + 2 * unit_no(half, b, g)
                            pe.wait_ge(z_kept, kept - 1 if before else kept)
                            mm = conv(half, b, g, 0)
                            if g == 3:
                                mm = tail(half, b)
                            mm.then_inc(conv_mm, 1)
                            if before:
                                mix(*before)
                            if (b, g) == (0, 0):
                                pe.wait_ge(m_ready, 2 * k2 + half + 1)
                            pe.wait_ge(z_kept, kept)
                            conv(half, b, g, 1).then_inc(conv_mm, 1)
                            before = (half, b, g)
                mix(*before)

            pe.wait_ge(mix_added, ONE + 4 * B * K)
            norm(2)
            pe.wait_ge(ln_out, ONE + 3 * NCH)
            for b in range(B):
                pe.wait_ge(sums_done, 2 * b + 2)
                if b:
                    pe.wait_ge(lines_kept, b)
                pe.matmul(bank[7][:, 0:H], WT[:, WM, :], sums[:, 0, b, :], start=True, stop=True)
                pe.matmul(bank[7][:, H:H + W], WT[:, WK_, :], sums[:, 1, b, :], start=True, stop=True
                          ).then_inc(lines_mm, 1)
                if b:
                    pe.wait_ge(msg_added, CPI * b)
                for r in range(CPI):
                    pe.matmul(bank[r][:, 0:CH], WT[:, WSELF, :], N[:, b * T + r * CH:b * T + (r + 1) * CH],
                              start=True, stop=True).then_inc(msg_mm, 1)

            pe.wait_ge(lines_added, B)
            norm(3)
            pe.wait_ge(ln_out, ONE + 4 * NCH)
            with pe.Fori(0, B) as b:
                pe.wait_ge(wx_stats, ONE + CPI * b)
                pe.wait_ge(wx_kept, ONE + CPI * b)
                for r in range(CPI):
                    pe.matmul(bank[r][:, 0:CH], WT[:, WR, :], N[:, ds(b * T + r * CH, CH)],
                              start=True, stop=True).then_inc(wx_mm, 1)

            def place(n, s, piece):
                if piece == 0:
                    pe.wait_ge(wx_normed, n + 1)
                a = piece * CH // 4
                mm = pe.matmul(bank[s][:, a:a + CH // 4], ident[:, :], wxn[:, s, a:a + CH // 4],
                               start=(piece == 0), stop=True, skip_group_check=True)
                if piece == 3:
                    mm.then_inc(wx_placed, 1)

            def turn(n, s, b):
                if b == 0:
                    pe.wait_ge(res_added, ONE + n + 1)
                    pe.wait_ge(res_kept, ONE + n)
                mm = pe.transpose(bank[4 + s][0:SB, b * C:(b + 1) * C], res[:, s, b * SB:(b + 1) * SB], ident[:, :])
                if b == B - 1:
                    mm.then_inc(res_turned, 1)

            def steps(n, s, first, last):
                for t in range(SB):
                    prev = ys[:, s, B * t - B:B * t] if t else ys[:, 1 - s, CH - B:CH]
                    if t or not first:
                        pe.wait_ge(y_ready, n * SB + t)
                    for o in range(0, C, C // 2):
                        mm = pe.matmul(bank[s][o:o + C // 2, B * t:B * t + B], WT[:, WV_R, o:o + C // 2], prev,
                                       start=False, stop=True, skip_group_check=True)
                    mm.then_inc(step_mm, 1)
                    if t % 20 == 0 and 20 <= t < 100 and not last:
                        place(n + 1, 1 - s, t // 20 - 1)
                    if t % 20 == 10 and t < 80 and not first:
                        turn(n - 1, 1 - s, t // 20)

            pe.wait_ge(wx_stats, ONE + NCH)
            pe.wait_ge(wx_kept, ONE + NCH)
            for piece in range(4):
                place(0, 0, piece)
            steps(0, 0, True, False)
            with pe.Fori(0, (NSB - 2) // 2) as n2:
                steps(2 * n2 + 1, 1, False, False)
                steps(2 * n2 + 2, 0, False, False)
            steps(NSB - 1, 1, False, True)
            for b in range(B):
                turn(NSB - 1, 1, b)

        @block.scalar
        def _(act):
            for signal in (o_kept, v_kept, p_kept_a, wx_kept):
                act.sem_inc(signal, ONE)
            act.wait_ge(c_loaded, 16 * 9)
            act.wait_ge(consts, 1)
            act.activation(ker[:, 5:6], ker[:, 0:1], ACT.Sqrt).then_inc(root_set, 1)
            act.wait_ge(root_set, 1)
            act.activation(ker[:, 5:6], ker[:, 5:6], ACT.Sqrt).then_inc(root_set, 1)
            act.wait_ge(dve_set, 3)
            act.activation(small[:, 20:24], small[:, 16:20], ACT.Exp).then_inc(exp_set, 1)

            for b in range(B):
                for g in range(0, CPI, 2):
                    act.wait_ge(x_turned, 7 * b + g + 1)
                    act.copy(X[:, b * T + g * CH:b * T + (g + 1) * CH], bank[g][:, 0:CH]).then_inc(x_kept_a, 1)
            def norm(ln, j):
                def squares(i):
                    act.wait_ge(ln_var, ONE + ln * NCH // 4 + i)
                    for u in range(4):
                        n = 4 * i + u
                        act.wait_ge(ln_diff, ONE + ln * NCH + n + 1)
                        act.activation(S1[:, u, :], N[:, ds(n * CH, CH)], ACT.Square).then_inc(ln_sq, 1)

                def deviations(i):
                    act.wait_ge(ln_rstd, ONE + ln * NCH // 4 + i)
                    act.wait_ge(ln_var, ONE + ln * NCH // 4 + i + 1)
                    act.activation(S2[:, 0, :], bank[4][:, 0:CH], ACT.Sqrt, bias=eps[:, j:j + 1]).then_inc(ln_std, 1)

                squares(0)
                with act.Fori(0, NCH // 4 - 1) as i:
                    deviations(i)
                    squares(i + 1)
                deviations(NCH // 4 - 1)

            norm(0, 0)

            act.wait_ge(pads_set, 1)
            with act.Fori(0, B) as b:
                act.wait_ge(qk_mm, ONE + 4 * TILES * b)
                for c in range(CPI):
                    act.wait_ge(qkv_mm, 21 * b + 3 * c + 2)
                    act.activation(kpad[:, PAD + 8 * c:PAD + 8 * c + 8, PAD:PAD + W],
                                   bank[2 + c % 2][:, 0:CH].rearrange("p (h w) -> p h w", w=W),
                                   ACT.Identity, bias=qkvb[:, 1:2]).then_inc(k_kept, 1)

                def exps(t):
                    s = t % 2
                    act.wait_ge(max_ready, TILES * b + t + 1)
                    act.wait_ge(rec_done, ONE + (TILES * b + t - 1 if t >= 2 else TILES * b))
                    for h in range(HEADS):
                        last = act.activation(logits[s][:, h, :], logits[s][:, h, :], ACT.Exp,
                                              bias=aneg[:, 4 * s + h:4 * s + h + 1],
                                              accum_out=aden[:, 4 * s + h:4 * s + h + 1])
                    last.then_inc(exp_done, 1)

                def keep_values(t):
                    act.wait_ge(v_turned, ONE + TILES * b + t + 1)
                    act.wait_ge(pv_mm, ONE + TILES * b + (t - 1 if t >= 2 else 0))
                    act.copy(v_win[0:120, t % 2, 0:2, :].rearrange("p c n -> p (c n)"), bank[6][0:120, 0:2 * C])
                    act.copy(v_win[0:40, t % 2, 2, :], bank[6][0:40, 2 * C:3 * C]).then_inc(v_kept, 1)

                def keep_probs(t):
                    act.wait_ge(p_turned, ONE + 3 * TILES * b + 3 * t + 3)
                    act.copy(probsT[0:40, t % 2, 2, :], bank[5][0:40, 0:CH]).then_inc(p_kept_a, 1)

                def keep_out(t):
                    r0, c0 = t // (W // QC) * QR, t % (W // QC) * QC
                    act.wait_ge(pv_mm, ONE + TILES * b + t + 1)
                    act.copy(N[:, :].rearrange("p (b h w) -> p b h w", b=B, h=H)[:, ds(b, 1), r0:r0 + QR, c0:c0 + QC],
                             bank[7][:, 0:TP].rearrange("p (b h w) -> p b h w", b=1, h=QR)
                             ).then_inc(o_kept, 1)

                exps(0)
                for t in range(TILES):
                    keep_values(t)
                    if t + 1 < TILES:
                        exps(t + 1)
                    if t:
                        keep_out(t - 1)
                    keep_probs(t)
                keep_out(TILES - 1)

            norm(1, 1)
            act.wait_ge(ln_out, ONE + 2 * NCH)
            with act.Fori(0, B) as b:
                def part(g):
                    k, n = (2, C) if g < UG else (1, TAIL)
                    act.wait_ge(u_turned, ONE + 7 * b + (g - 1 if g >= 2 else 0))
                    backwards = bass.AP(SIDE, g % 2 * 512 + n - 1, [[SIDE_W, C], [2 * n, k], [n, 2], [-1, n]])
                    act.copy(backwards, N[:, ds(b * T + g * 4 * C, 2 * k * n)].rearrange("p (n i q) -> p n q i", n=k, q=2)
                             ).then_inc(u_parted, 1)

                def high(g):
                    n, w = (C, 512) if g < UG else (TAIL, 256)
                    act.wait_ge(u_turned, ONE + 7 * b + g + 1)
                    act.activation(u16[0:n, 0, ds(b, 1)].rearrange("p b n q d -> p (b n q d)")[:, g * 512:g * 512 + w],
                                   bank[4 + g % 4][0:n, 0:w], ACT.Copy, scale=U_SCALE).then_inc(u_hi, 1)
                    if g < UG:
                        act.wait_ge(x_lo, ONE + 6 * b + (g - 1 if g >= 2 else 0))
                        act.copy(u_sum[:, g % 2], bank[4 + g % 4][:, 0:2 * C]).then_inc(u_first, 1)

                part(0)
                for g in range(7):
                    if g < 6:
                        part(g + 1)
                    high(g)
            with act.Fori(0, K * B) as image:
                for g in range(4):
                    unit = 4 * image + g
                    for e in range(2):
                        act.wait_ge(conv_mm, 2 * unit + e + 1)
                        if e == 0:
                            act.wait_ge(mix_mm, ONE + unit)
                        if g == 3 and e == 0:
                            act.copy(z_tail.rearrange("p e n -> p (e n)"), bank[0][:, CU:CU + 4 * TAIL])
                        act.copy(zs[:, e], bank[3 * e][:, 0:CU].unsqueeze(1).broadcast_to([C, 2, CU])
                                 ).then_inc(z_shared, 1)

            norm(2, 0)
            for b in range(B):
                act.wait_ge(lines_mm, b + 1)
                act.copy(lines[:, b, :], bank[7][:, 0:H + W]).then_inc(lines_kept, 1)
            norm(3, 1)
            with act.Fori(0, B) as b:
                for r in range(CPI):
                    act.wait_ge(wx_mm, CPI * b + r + 1)
                    act.copy(wx[:, r * CH:(r + 1) * CH, ds(b, 1)],
                             bank[r][:, 0:CH].unsqueeze(2)).then_inc(wx_kept, 1)

            act.wait_ge(bn_step, 1)
            act.activation(bn[:, 2:3], bn[:, 1:2], ACT.Sqrt, bias=eps[:, 1:2]).then_inc(bn_step, 1)

            def steps(n, s):
                if not (isinstance(n, int) and n == 0):
                    act.wait_ge(res_added, ONE + n - 1)
                for t in range(SB):
                    act.wait_ge(step_mm, n * SB + t + 1)
                    act.activation(ys[:, s, B * t:B * t + B], bank[s][:, B * t:B * t + B],
                                   ACT.Sigmoid).then_inc(y_ready, 1)

            steps(0, 0)
            with act.Fori(0, (NSB - 2) // 2) as n2:
                steps(2 * n2 + 1, 1)
                steps(2 * n2 + 2, 0)
            steps(NSB - 1, 1)

        @block.vector
        def _(dve):
            for signal in (ln_diff, ln_rstd, ln_out, attn_added, p_kept_v, ar_added, u_lo, x_lo, z_kept, mix_added, wx_stats, rec_done, res_kept):
                dve.sem_inc(signal, ONE)
            count = [0]

            def link(ins):
                count[0] += 1
                ins.then_inc(dve_set, 1)
                dve.wait_ge(dve_set, count[0])

            dve.wait_ge(c_loaded, 16 * 9)
            link(dve.tensor_tensor(small[:, 8:12], small[:, 0:4], small[:, 4:8], ALU.add))
            link(dve.tensor_reduce(small[:, 12:13], small[:, 8:12], AX.X, ALU.max))
            link(dve.tensor_scalar(small[:, 16:20], small[:, 8:12], small[:, 12:13], None, ALU.subtract))
            for n in range(3):
                k = 4 if n < 2 else 1
                dve.wait_ge(w_turned, n + 1)
                dve.tensor_copy(WT[:, 4 * n:4 * n + k, :].rearrange("p n c -> p (n c)"),
                                bank[n][:, 0:k * C]).then_inc(w_kept, 1)
            for g in range(CPI):
                dve.wait_ge(phi_turned, g + 1)
                dve.tensor_copy(phiT[:, g * CH:(g + 1) * CH], bank[3 + g % 4][0:K, 0:CH]).then_inc(phi_kept, 1)
            dve.wait_ge(phi_kept, CPI)
            link(dve.memset(taps[:, :, :, 0:C], 0.0))
            link(dve.tensor_reduce(ker[:, 1:2], phiT, AX.X, ALU.max, apply_absolute_value=True))
            link(dve.tensor_scalar(ker[:, 2:3], ker[:, 1:2], 1e-30, None, ALU.max))
            link(dve.reciprocal(ker[:, 3:4], ker[:, 2:3]))
            link(dve.tensor_scalar(ker[:, 4:5], ker[:, 3:4], PHI_SCALE, None, ALU.mult))
            for q in range(2):
                link(dve.tensor_scalar(taps[:, 0, q, C:], phiT[:, q::2], ker[:, 4:5], None, ALU.mult))
            for q in range(2):
                last = dve.scalar_tensor_tensor(out=taps[:, 1, q, C:], in0=phiT[:, q::2], scalar=ker[:, 4:5],
                                                in1=taps[:, 0, q, C:], op0=ALU.mult, op1=ALU.subtract)
            last.then_inc(taps_split, 1)
            link(dve.memset(diffs[:, :, :, 0:C], 0.0))
            for q in range(2):
                phi_q = phiT[:, q::2]
                dve.tensor_scalar(diff_raw[:, 0:C], phi_q[:, 0:C], -1.0, None, ALU.mult)
                link(dve.tensor_tensor(diff_raw[:, C:], phi_q[:, 0:L - C], phi_q[:, C:], ALU.subtract))
                link(dve.tensor_scalar(diffs[:, 0, q, C:], diff_raw, ker[:, 4:5], None, ALU.mult))
                dve.scalar_tensor_tensor(out=diffs[:, 1, q, C:], in0=diff_raw, scalar=ker[:, 4:5],
                                         in1=diffs[:, 0, q, C:], op0=ALU.mult, op1=ALU.subtract
                                         ).then_inc(diffs_split, 1)
                dve.wait_ge(diffs_split, q + 1)
            dve.wait_ge(root_set, 2)
            link(dve.tensor_scalar(ker[:, 6:7], ker[:, 2:3], 1.0 / (PHI_SCALE * U_SCALE), None, ALU.mult))
            link(dve.tensor_tensor(ker[:, 7:8], ker[:, 5:6], ker[:, 6:7], ALU.mult))
            dve.wait_ge(consts, 1)
            dve.tensor_scalar(diag16[:, :], ident[0:K, 0:K], ker[:, 7:8], None, ALU.mult).then_inc(diag_set, 1)
            for b in range(B):
                for g in range(1, CPI, 2):
                    dve.wait_ge(x_turned, 7 * b + g + 1)
                    dve.tensor_copy(X[:, b * T + g * CH:b * T + (g + 1) * CH], bank[g][:, 0:CH]).then_inc(x_kept_v, 1)
            dve.wait_ge(sk_spread, 1)
            link(dve.tensor_copy(sk[:, :], bank[7][:, 0:K]))
            dve.wait_ge(exp_set, 1)
            link(dve.tensor_reduce(small[:, 24:25], small[:, 20:24], AX.X, ALU.add))
            link(dve.reciprocal(small[:, 25:26], small[:, 24:25]))
            link(dve.tensor_scalar(small[:, 28:32], small[:, 20:24], small[:, 25:26], None, ALU.mult))
            link(dve.tensor_reduce(small[:, 32:33], small[:, 28:32], AX.X, ALU.max))
            link(dve.tensor_scalar(small[:, 36:40], small[:, 28:32], small[:, 32:33], None, ALU.is_equal))
            link(dve.tensor_scalar(small[:, 40:44], small[:, 36:40], -1.0, 1.0, ALU.mult, ALU.add))
            link(dve.memset(small[:, 44:45], 1.0))
            for i in range(1, EXPERTS):
                link(dve.tensor_tensor(small[:, 44 + i:45 + i], small[:, 43 + i:44 + i], small[:, 39 + i:40 + i], ALU.mult))
            link(dve.tensor_tensor(small[:, 48:52], small[:, 36:40], small[:, 44:48], ALU.mult))
            link(dve.tensor_tensor(small[:, 52:56], small[:, 48:52], small[:, 28:32], ALU.subtract))
            link(dve.tensor_tensor(small[:, 56:60], small[:, 52:56], small[:, 28:32], ALU.add))
            for i in range(EXPERTS):
                dve.tensor_scalar(wsk[:, i, :], sk[:, :], small[:, 56 + i:57 + i], None, ALU.mult)
            dve.wait_ge(mu_loaded, 16)
            link(dve.tensor_scalar(Mu_eff[:, 0], mu_raw[:, 0], small[:, 56:57], None, ALU.mult))
            for i in range(1, EXPERTS):
                link(dve.scalar_tensor_tensor(out=Mu_eff[:, i], in0=mu_raw[:, i], scalar=small[:, 56 + i:57 + i],
                                              in1=Mu_eff[:, i - 1], op0=ALU.mult, op1=ALU.add))
            dve.memset(bn[:, 7:8], 0.0).then_inc(gates, 1)

            def norm(ln):
                def centre(i):
                    for u in range(4):
                        n = 4 * i + u
                        dve.wait_ge(ln_mean, ln * NCH + n + 1)
                        dve.tensor_tensor(N[:, ds(n * CH, CH)], X[:, ds(n * CH, CH)], bank[u][:, 0:CH],
                                          ALU.subtract).then_inc(ln_diff, 1)

                def invert(i):
                    dve.wait_ge(ln_std, ln * NCH // 4 + i + 1)
                    dve.reciprocal(S2[:, 1, :], S2[:, 0, :]).then_inc(ln_rstd, 1)

                def scale(i):
                    for u in range(4):
                        n = 4 * i + u
                        dve.wait_ge(ln_spread, ln * NCH + n + 1)
                        dve.tensor_tensor(N[:, ds(n * CH, CH)], N[:, ds(n * CH, CH)], bank[5 + u % 3][:, 0:CH],
                                          ALU.mult).then_inc(ln_out, 1)

                centre(0)
                with dve.Fori(0, NCH // 4 - 1) as i:
                    invert(i)
                    centre(i + 1)
                    scale(i)
                invert(NCH // 4 - 1)
                scale(NCH // 4 - 1)

            dve.wait_ge(taps_stored, 32)
            norm(0)

            dve.wait_ge(pads_set, 1)
            dve.wait_ge(bias_loaded, 16 * HEADS * QR)
            with dve.Fori(0, B) as b:
                dve.wait_ge(qk_mm, ONE + 4 * TILES * b)
                dve.wait_ge(v_turned, ONE + TILES * b)
                for c in range(CPI):
                    dve.wait_ge(qkv_mm, 21 * b + 3 * c + 1)
                    dve.tensor_scalar(qT[:, 4 * c:4 * c + 4, :].rearrange("p t (i j) -> p i t j", i=QR),
                                      bank[c % 2][:, 0:CH].rearrange("p (i t j) -> p i t j", i=QR, t=4),
                                      qkvb[:, 0:1], SCALE, ALU.add, ALU.mult).then_inc(qv_kept, 1)
                    dve.wait_ge(qkv_mm, 21 * b + 3 * c + 3)
                    dve.tensor_scalar(vpad[:, PAD + 8 * c:PAD + 8 * c + 8, PAD:PAD + W],
                                      bank[4 + c % 2][:, 0:CH].rearrange("p (h w) -> p h w", w=W),
                                      qkvb[:, 2:3], None, ALU.add).then_inc(qv_kept, 1)

                def row_max(t):
                    s = t % 2
                    dve.wait_ge(p_turned, ONE + 3 * TILES * b + (3 * t - 3 if t >= 2 else 0))
                    for h in range(HEADS):
                        dve.wait_ge(qk_mm, ONE + 4 * TILES * b + 4 * t + h + 1)
                        dve.memset(waited[:, h:h + 1], 0.0)
                        dve.tensor_tensor_reduce(out=logits[s][:, h, :], in0=bank[(HEADS * t + h) % 3][0:TP, 0:NK], in1=wbias[:, h, :],
                                                 scale=1.0, scalar=-3.0e38, op0=ALU.add, op1=ALU.max,
                                                 accum_out=amax[:, 4 * s + h:4 * s + h + 1]).then_inc(biased, 1)
                    dve.wait_ge(biased, 4 * TILES * b + 4 * t + 4)
                    dve.tensor_scalar(aneg[:, 4 * s:4 * s + 4], amax[:, 4 * s:4 * s + 4], -1.0, None,
                                      ALU.mult).then_inc(max_ready, 1)

                row_max(0)
                for t in range(TILES):
                    s = t % 2
                    dve.wait_ge(exp_done, TILES * b + t + 1)
                    dve.reciprocal(arec, aden[:, 4 * s:4 * s + 4]).then_inc(rec_done, 1)
                    dve.wait_ge(rec_done, ONE + TILES * b + t + 1)
                    dve.tensor_tensor(diag[:, s], ident[0:TP, 0:TP].unsqueeze(1).broadcast_to([TP, HEADS, TP]),
                                      arec.unsqueeze(2).broadcast_to([TP, HEADS, TP]), ALU.mult).then_inc(diag_ready, 1)
                    if t + 1 < TILES:
                        row_max(t + 1)
                    dve.wait_ge(pv_mm, ONE + TILES * b + (t - 1 if t >= 2 else 0))
                    for c in range(2):
                        dve.wait_ge(p_turned, ONE + 3 * TILES * b + 3 * t + c + 1)
                        dve.tensor_copy(probsT[0:120, s, c, :], bank[3 + c][0:120, 0:CH]).then_inc(p_kept_v, 1)
                for c in range(CPI):
                    dve.wait_ge(proj_mm, CPI * b + c + 1)
                    xs = X[:, ds(b * T + c * CH, CH)]
                    dve.scalar_tensor_tensor(out=xs, in0=bank[4 + c % 2][:, 0:CH], scalar=projb[:, 0:1], in1=xs,
                                             op0=ALU.add, op1=ALU.add).then_inc(attn_added, 1)

            norm(1)
            with dve.Fori(0, B) as b:
                for s in range(8):
                    dve.wait_ge(ar_mm, 8 * b + s + 1)
                    xs = X[:, ds(b * T + s * CC, CC)]
                    dve.tensor_tensor(xs, xs, bank[s % 4][:, 0:CC], ALU.add).then_inc(ar_added, 1)
                    if s < UG:
                        dve.wait_ge(u_first, 6 * b + s + 1)
                        dve.tensor_tensor(u_sum[:, s % 2], u_sum[:, s % 2], bank[4 + s % 4][:, 2 * C:4 * C],
                                          ALU.add).then_inc(u_summed, 1)
                    if s < UG + 1:
                        n, w = (C, 512) if s < UG else (TAIL, 256)
                        dve.wait_ge(u_hi, 7 * b + s + 1)
                        hi, lo = (u16[0:n, h, ds(b, 1)].rearrange("p b n q d -> p (b n q d)")[:, s * 512:s * 512 + w]
                                  for h in range(2))
                        dve.scalar_tensor_tensor(out=lo, in0=bank[4 + s % 4][0:n, 0:w], scalar=U_SCALE, in1=hi,
                                                 op0=ALU.mult, op1=ALU.subtract).then_inc(u_lo, 1)
                    if s < UG:
                        hi, lo = (x16[:, h, ds(b, 1), s].rearrange("p b q d -> p (b q d)") for h in range(2))
                        dve.wait_ge(u_summed, 6 * b + s + 1)
                        dve.tensor_scalar(hi, u_sum[:, s % 2], U_SCALE, None, ALU.mult).then_inc(x_hi, 1)
                        dve.wait_ge(x_hi, 6 * b + s + 1)
                        dve.scalar_tensor_tensor(out=lo, in0=u_sum[:, s % 2], scalar=U_SCALE, in1=hi,
                                                 op0=ALU.mult, op1=ALU.subtract).then_inc(x_lo, 1)
            with dve.Fori(0, K) as k:
                with dve.Fori(0, B) as b:
                    first = 4 * (B * k + b)
                    image = X[:, ds(b * T, T)]

                    def keep(g, e):
                        dve.wait_ge(z_shared, 2 * (first + g) + e + 1)
                        dve.tensor_tensor(zs[:, e, 0, :], zs[:, e, 0, :], bank[3 * e + 1][:, 0:CU], ALU.add)
                        dve.tensor_tensor(zs[:, e, 1, :], zs[:, e, 1, :], bank[3 * e + 2][:, 0:CU],
                                          ALU.subtract).then_inc(z_kept, 1)

                    def add(g):
                        p, h = unit_of(g)
                        dve.wait_ge(mix_mm, ONE + first + g + 1)
                        if g == 3:
                            xs = X[:, ds(b * T + 2 * SPAN, 2 * TAIL)].rearrange("p (t q) -> p q t", q=2)
                            dve.tensor_tensor(xs, xs, bank[6][:, CU:CU + 2 * TAIL].rearrange("p (q t) -> p q t", q=2),
                                              ALU.add)
                        for a in range(2):
                            xs = X[:, ds(b * T + h * SPAN, SPAN)].rearrange(
                                "p (i a t q) -> p a q i t", i=PH, a=2, q=2)[:, a, p]
                            last = dve.tensor_tensor(xs, xs, bank[6 + a][:, 0:CU].rearrange("p (i t) -> p i t", i=PH),
                                                     ALU.add)
                        last.then_inc(mix_added, 1)

                    for g in range(4):
                        keep(g, 0)
                        if g:
                            add(g - 1)
                        keep(g, 1)
                    add(3)

            norm(2)
            dve.wait_ge(ln_out, ONE + 3 * NCH)
            grid = N[:, :].rearrange("p (b h w) -> p b h w", b=B, h=H)

            def line_sums(b):
                dve.tensor_reduce(sums[:, 0, b, :], grid[:, b], AX.X, ALU.add).then_inc(sums_done, 1)
                dve.tensor_reduce(sums[:, 1, b, :], grid[:, b].rearrange("p h w -> p w h"), AX.X,
                                  ALU.add).then_inc(sums_done, 1)

            def add_lines(b):
                dve.wait_ge(lines_spread, b + 1)
                dve.wait_ge(msg_added, CPI * b + CPI)
                xs = X[:, b * T:(b + 1) * T]
                dve.tensor_tensor(xs, xs, N[:, b * T:(b + 1) * T], ALU.add).then_inc(lines_added, 1)

            line_sums(0)
            for b in range(B):
                if b + 1 < B:
                    line_sums(b + 1)
                for r in range(CPI):
                    dve.wait_ge(msg_mm, CPI * b + r + 1)
                    xs = X[:, b * T + r * CH:b * T + (r + 1) * CH]
                    dve.tensor_tensor(xs, xs, bank[r][:, 0:CH], ALU.add).then_inc(msg_added, 1)
                if b:
                    add_lines(b - 1)
            add_lines(B - 1)

            norm(3)
            with dve.Fori(0, B) as b:
                for r in range(CPI):
                    dve.wait_ge(wx_kept, ONE + CPI * b + r + 1)
                    dve.bn_stats(stats[:, ds(CPI * b + r, 1), :], bank[r][:, 0:CH]).then_inc(wx_stats, 1)
            dve.wait_ge(wx_stats, ONE + NCH)
            dve.bn_aggr(bn[:, 0:2], stats[:, :, :].rearrange("p n s -> p (n s)")).then_inc(bn_step, 1)
            dve.wait_ge(bn_step, 2)
            link(dve.reciprocal(bn[:, 6:7], bn[:, 2:3]))
            link(dve.tensor_tensor(bn[:, 3:4], gb[:, 0:1], bn[:, 6:7], ALU.mult))
            link(dve.tensor_tensor(bn[:, 4:5], bn[:, 0:1], bn[:, 3:4], ALU.mult))
            link(dve.tensor_tensor(bn[:, 5:6], gb[:, 1:2], bn[:, 4:5], ALU.subtract))
            link(dve.memset(ys[:, 1, CH - B:CH], 0.0))
            dve.wait_ge(wx_kept, ONE + NCH)

            def scaled(n, s):
                dve.tensor_scalar(wxn[:, s, :].rearrange("p (t b) -> p t b", b=B), wx[:, ds(n * SB, SB), :],
                                  bn[:, 3:4], bn[:, 5:6], ALU.mult, ALU.add).then_inc(wx_normed, 1)

            def keep(m, s):
                dve.wait_ge(res_turned, ONE + m + 1)
                if not (isinstance(m, int) and m < 2):
                    dve.wait_ge(stored[s], 8 * (m - s))
                dve.tensor_copy(o_out[:, s].rearrange("p b c -> p (b c)"), bank[4 + s][0:SB, :]).then_inc(res_kept, 1)

            scaled(0, 0)
            scaled(1, 1)
            for n in range(2):
                dve.wait_ge(wx_placed, n + 1)
                scaled(n + 2, n)
                keep(n, n)
            with dve.Fori(1, (NSB - 2) // 2) as n2:
                for s in range(2):
                    n = 2 * n2 + s
                    dve.wait_ge(wx_placed, n + 1)
                    scaled(n + 2, s)
                    keep(n, s)
            keep(NSB - 2, 0)
            keep(NSB - 1, 1)


_INS = ["x", "L0_conv_qkv_w", "L0_conv_qkv_b", "L0_conv_rpb", "L0_conv_proj_w", "L0_conv_proj_b", "L0_ffn_sigma",
        "L0_ffn_phi", "L0_ffn_M_u", "L0_ffn_M_phi_plus", "L0_ffn_M_phi_minus", "L0_ffn_log_weights", "L0_ffn_gumbel",
        "L1_conv_Wself", "L1_conv_Wm", "L1_conv_Wk", "L1_ffn_W", "L1_ffn_V", "L1_ffn_gamma", "L1_ffn_beta"]


def kernel(**inputs):
    import numpy as _np
    import concourse.bacc as _bacc
    from concourse import mybir as _mybir
    from concourse.bass_utils import run_bass_kernel_spmd as _run

    nc = _bacc.Bacc("TRN2", target_bir_lowering=False, num_devices=1)
    arrays, args = {}, []
    for name in _INS:
        a = _np.ascontiguousarray(inputs[name])
        arrays[f"in_{name}_dram"] = a
        args.append(nc.dram_tensor(f"in_{name}_dram", a.shape, _mybir.dt.from_np(a.dtype), kind="ExternalInput").ap())
    args.append(nc.dram_tensor("out_0_dram", (B, H, W, C), F32, kind="ExternalOutput").ap())
    build(nc, *args)
    r = _run(nc, [arrays], core_ids=[0])
    return r.results[0]["out_0_dram"]
```
